# Optimizing a Trainium2 kernel written in Bass

```python
import numpy as np
import jax
import jax.numpy as jnp

def _softmax(x, axis=-1):
    return jax.nn.softmax(x, axis=axis)

def _gelu(x):
    return jax.nn.gelu(x, approximate=True)

def _silu(x):
    return jax.nn.silu(x)

def _sigmoid(x):
    return jax.nn.sigmoid(x)

def _layernorm(x, axis=-1, eps=1e-05):
    m = jnp.mean(x, axis=axis, keepdims=True)
    v = jnp.var(x, axis=axis, keepdims=True)
    return (x - m) / jnp.sqrt(v + eps)

def _scatter_add(tgt, idx, src, axis=0):
    return tgt.at[idx].add(src)

def _segment_sum(src, seg, n):
    return jax.ops.segment_sum(src, seg, n)
kernel_name = 'mk_recurrent_d1_jaxref_r8_e57d2d'

def setup_inputs(seed: int=0):
    np.random.seed(seed)
    _w = jnp.asarray

    def _L0_attn_setup():
        import math
        import jax, jax.numpy as jnp
        import numpy as np
        B, T, E = (2, 256, 256)
        NUM_HEADS = 16
        H = NUM_HEADS // 2
        D = E // NUM_HEADS
        DEPTH = 12
        LAMBDA_INIT = 0.8 - 0.6 * math.exp(-0.3 * DEPTH)
        EPS = 1e-05

        def _forward(x, Wq, Wk, Wv, Wo, lq1, lk1, lq2, lk2, g):
            Bz, Tl, _ = x.shape
            q = (x @ Wq).reshape(Bz, Tl, H, 2, D)
            k = (x @ Wk).reshape(Bz, Tl, H, 2, D)
            v = (x @ Wv).reshape(Bz, Tl, H, 2 * D)
            scale = D ** (-0.5)
            causal = jnp.tril(jnp.ones((Tl, Tl), dtype=bool))

            def attend(qc, kc):
                s = jnp.einsum('bthd,bshd->bhts', qc, kc) * scale
                s = jnp.where(causal, s, -jnp.inf)
                a = jax.nn.softmax(s, axis=-1)
                return jnp.einsum('bhts,bshe->bthe', a, v)
            o1 = attend(q[..., 0, :], k[..., 0, :])
            o2 = attend(q[..., 1, :], k[..., 1, :])
            lam = jnp.exp(jnp.sum(lq1 * lk1)) - jnp.exp(jnp.sum(lq2 * lk2)) + LAMBDA_INIT
            o = o1 - lam * o2
            o = o * jax.lax.rsqrt(jnp.mean(o * o, axis=-1, keepdims=True) + EPS) * g
            o = o * (1.0 - LAMBDA_INIT)
            return o.reshape(Bz, Tl, E) @ Wo
        key = jax.random.key(seed)
        ks = jax.random.split(key, 10)
        sc = lambda k, shape, std: jax.random.normal(k, shape, dtype=jnp.float32) * std
        return {'x': jax.random.normal(ks[0], (B, T, E), dtype=jnp.float32), 'Wq': sc(ks[1], (E, E), 0.02), 'Wk': sc(ks[2], (E, E), 0.02), 'Wv': sc(ks[3], (E, E), 0.02), 'Wo': sc(ks[4], (E, E), 0.02), 'lambda_q1': sc(ks[5], (D,), 0.1), 'lambda_k1': sc(ks[6], (D,), 0.1), 'lambda_q2': sc(ks[7], (D,), 0.1), 'lambda_k2': sc(ks[8], (D,), 0.1), 'g': jnp.ones((2 * D,), dtype=jnp.float32)}
    _L0_attn_in = _L0_attn_setup()

    def _L0_ffn_setup():
        import jax, jax.numpy as jnp
        import numpy as np
        DIM = 256
        INTER = 176
        E = 16
        TOPK = 4
        G = 4
        TOPK_G = 2
        N_SHARED = 2
        ROUTE_SCALE = 1.0
        INIT_STD = 0.02
        B, S = (1, 256)
        key = jax.random.key(seed)
        ks = jax.random.split(key, 9)
        std = INIT_STD
        x = jax.random.normal(ks[0], (B, S, DIM), jnp.float32)
        gate_w = jax.random.normal(ks[1], (E, DIM), jnp.float32) * std
        expert_bias = jnp.zeros((E,), jnp.float32)
        w1 = jax.random.normal(ks[2], (E, DIM, INTER), jnp.float32) * std
        w3 = jax.random.normal(ks[3], (E, DIM, INTER), jnp.float32) * std
        w2 = jax.random.normal(ks[4], (E, INTER, DIM), jnp.float32) * std
        sh = N_SHARED * INTER
        sw1 = jax.random.normal(ks[5], (DIM, sh), jnp.float32) * std
        sw3 = jax.random.normal(ks[6], (DIM, sh), jnp.float32) * std
        sw2 = jax.random.normal(ks[7], (sh, DIM), jnp.float32) * std
        return {'x': x, 'gate_w': gate_w, 'expert_bias': expert_bias, 'w1': w1, 'w2': w2, 'w3': w3, 'sw1': sw1, 'sw2': sw2, 'sw3': sw3}
    _L0_ffn_in = _L0_ffn_setup()
    _d = {'L0_attn_x': _L0_attn_in['x'], 'L0_attn_Wq': _L0_attn_in['Wq'], 'L0_attn_Wk': _L0_attn_in['Wk'], 'L0_attn_Wv': _L0_attn_in['Wv'], 'L0_attn_Wo': _L0_attn_in['Wo'], 'L0_attn_lambda_q1': _L0_attn_in['lambda_q1'], 'L0_attn_lambda_k1': _L0_attn_in['lambda_k1'], 'L0_attn_lambda_q2': _L0_attn_in['lambda_q2'], 'L0_attn_lambda_k2': _L0_attn_in['lambda_k2'], 'L0_attn_g': _L0_attn_in['g'], 'L0_ffn_gate_w': _L0_ffn_in['gate_w'], 'L0_ffn_expert_bias': _L0_ffn_in['expert_bias'], 'L0_ffn_w1': _L0_ffn_in['w1'], 'L0_ffn_w2': _L0_ffn_in['w2'], 'L0_ffn_w3': _L0_ffn_in['w3'], 'L0_ffn_sw1': _L0_ffn_in['sw1'], 'L0_ffn_sw2': _L0_ffn_in['sw2'], 'L0_ffn_sw3': _L0_ffn_in['sw3']}
    _x0 = _d['L0_attn_x']
    _d['L0_attn_x'] = jax.random.normal(jax.random.fold_in(jax.random.key(seed), 1), (1, 1024, 256), dtype=_x0.dtype)
    del _x0
    return _d

def reference(L0_attn_x, L0_attn_Wq, L0_attn_Wk, L0_attn_Wv, L0_attn_Wo, L0_attn_lambda_q1, L0_attn_lambda_k1, L0_attn_lambda_q2, L0_attn_lambda_k2, L0_attn_g, L0_ffn_gate_w, L0_ffn_expert_bias, L0_ffn_w1, L0_ffn_w2, L0_ffn_w3, L0_ffn_sw1, L0_ffn_sw2, L0_ffn_sw3):

    def _L0_attn_ref(x, Wq, Wk, Wv, Wo, lambda_q1, lambda_k1, lambda_q2, lambda_k2, g):
        import math
        import jax, jax.numpy as jnp
        import numpy as np
        B, T, E = (2, 256, 256)
        NUM_HEADS = 16
        H = NUM_HEADS // 2
        D = E // NUM_HEADS
        DEPTH = 12
        LAMBDA_INIT = 0.8 - 0.6 * math.exp(-0.3 * DEPTH)
        EPS = 1e-05

        def _forward(x, Wq, Wk, Wv, Wo, lq1, lk1, lq2, lk2, g):
            Bz, Tl, _ = x.shape
            q = (x @ Wq).reshape(Bz, Tl, H, 2, D)
            k = (x @ Wk).reshape(Bz, Tl, H, 2, D)
            v = (x @ Wv).reshape(Bz, Tl, H, 2 * D)
            scale = D ** (-0.5)
            causal = jnp.tril(jnp.ones((Tl, Tl), dtype=bool))

            def attend(qc, kc):
                s = jnp.einsum('bthd,bshd->bhts', qc, kc) * scale
                s = jnp.where(causal, s, -jnp.inf)
                a = jax.nn.softmax(s, axis=-1)
                return jnp.einsum('bhts,bshe->bthe', a, v)
            o1 = attend(q[..., 0, :], k[..., 0, :])
            o2 = attend(q[..., 1, :], k[..., 1, :])
            lam = jnp.exp(jnp.sum(lq1 * lk1)) - jnp.exp(jnp.sum(lq2 * lk2)) + LAMBDA_INIT
            o = o1 - lam * o2
            o = o * jax.lax.rsqrt(jnp.mean(o * o, axis=-1, keepdims=True) + EPS) * g
            o = o * (1.0 - LAMBDA_INIT)
            return o.reshape(Bz, Tl, E) @ Wo
        return _forward(x, Wq, Wk, Wv, Wo, lambda_q1, lambda_k1, lambda_q2, lambda_k2, g)

    def _L0_ffn_ref(x, gate_w, expert_bias, w1, w2, w3, sw1, sw2, sw3):
        import jax, jax.numpy as jnp
        import numpy as np
        DIM = 256
        INTER = 176
        E = 16
        TOPK = 4
        G = 4
        TOPK_G = 2
        N_SHARED = 2
        ROUTE_SCALE = 1.0
        INIT_STD = 0.02
        B, S = (1, 256)
        b, s, d = x.shape
        T = b * s
        xf = x.reshape(T, d)
        scores = jax.nn.sigmoid(xf @ gate_w.T)
        original_scores = scores
        scores = scores + expert_bias
        sg = scores.reshape(T, G, E // G)
        group_scores = sg.max(axis=-1)
        _, gidx = jax.lax.top_k(group_scores, TOPK_G)
        gmask = jnp.zeros((T, G), bool).at[jnp.arange(T)[:, None], gidx].set(True)
        masked = jnp.where(gmask[:, :, None], sg, -jnp.inf).reshape(T, E)
        _, idx = jax.lax.top_k(masked, TOPK)
        w = jnp.take_along_axis(original_scores, idx, axis=1)
        w = w / jnp.sum(w, axis=-1, keepdims=True)
        w = w * ROUTE_SCALE
        cw = jnp.zeros((T, E), x.dtype).at[jnp.arange(T)[:, None], idx].add(w)
        h = jax.nn.silu(jnp.einsum('td,edh->teh', xf, w1)) * jnp.einsum('td,edh->teh', xf, w3)
        y = jnp.einsum('teh,ehd,te->td', h, w2, cw)
        z = jax.nn.silu(xf @ sw1) * (xf @ sw3) @ sw2
        return (y + z).reshape(b, s, d)
    x = L0_attn_x
    xn = _layernorm(x, axis=-1)
    s = _L0_attn_ref(xn, L0_attn_Wq, L0_attn_Wk, L0_attn_Wv, L0_attn_Wo, L0_attn_lambda_q1, L0_attn_lambda_k1, L0_attn_lambda_q2, L0_attn_lambda_k2, L0_attn_g)
    g = _silu(_L0_ffn_ref(xn, L0_ffn_gate_w, L0_ffn_expert_bias, L0_ffn_w1, L0_ffn_w2, L0_ffn_w3, L0_ffn_sw1, L0_ffn_sw2, L0_ffn_sw3))
    x = x + s * g
    return x

_drawn_inputs = setup_inputs


def setup_inputs(seed=0):
    import zlib

    import numpy as np

    out = dict(_drawn_inputs(seed))
    spreads = {'L0_attn_g': (1.0, 0.6), 'L0_ffn_expert_bias': (0.0, 0.8)}
    factors = {'L0_attn_Wq': 8.0,
     'L0_attn_Wk': 8.0,
     'L0_attn_Wv': 8.0,
     'L0_attn_Wo': 8.0,
     'L0_attn_lambda_q1': 8.0,
     'L0_attn_lambda_k1': 8.0,
     'L0_attn_lambda_q2': 8.0,
     'L0_attn_lambda_k2': 8.0,
     'L0_ffn_gate_w': 8.0,
     'L0_ffn_w1': 8.0,
     'L0_ffn_w2': 8.0,
     'L0_ffn_w3': 8.0,
     'L0_ffn_sw1': 8.0,
     'L0_ffn_sw2': 8.0,
     'L0_ffn_sw3': 8.0}
    for name, (base, spread) in spreads.items():
        noise = np.random.default_rng([zlib.crc32(name.encode()), seed]).standard_normal(out[name].shape)
        drawn = base * np.exp(spread * noise) if base else spread * noise
        out[name] = jnp.asarray(drawn.astype(out[name].dtype))
    for name, factor in factors.items():
        out[name] = (out[name] * factor).astype(out[name].dtype)
    return out
```

```python
import math
from contextlib import ExitStack

import concourse.bass as bass
from concourse import mybir

F32 = mybir.dt.float32
F32R = mybir.dt.float32r
BF16 = mybir.dt.bfloat16
ALU = mybir.AluOpType
ACT = mybir.ActivationFunctionType
X = mybir.AxisListType.X

P = 128
BANK = 512
T = 1024
E = 256
NT = T // P
KH = E // P
HEADS = 8
D = 16
DV = 2 * D
HALVES = 2
TH = T // HALVES
HH = HEADS // HALVES
EXPERTS, GROUPS, TOPK, TOPG = 16, 4, 4, 2
PER_GROUP = EXPERTS // GROUPS
INTER = 176
SHARED = 2 * INTER
ROUTED = EXPERTS * INTER
Q = P // EXPERTS
RTILES = INTER // Q
SH_SIZES = [P, P, SHARED - 2 * P]
SHT = len(SH_SIZES)
UNITS = SHT + RTILES
LAMBDA_INIT = 0.8 - 0.6 * math.exp(-0.3 * 12)
EPS = 1e-5
BIG = 3.0e38

Q_PART = [0, 0, 1, 1, 0, 2]
K_PART = [0, 1, 0, 1, 2, 0]
STACK = len(Q_PART) * D
STACK_DMAS = 16 * 2 * len(Q_PART)

ORDER = [7, 0, 6, 1, 5, 2, 4, 3]
STEPS = HH * NT
GROUP_OF = [1 + (ORDER[s % NT] >= 4) for s in range(STEPS)]
FIRST_GROUP = [sum(GROUP_OF[:s]) for s in range(STEPS)]
GPH = sum(GROUP_OF)

PIECES = 6
CHUNKS = PIECES * (UNITS + 1)
PHASES = STEPS + 2
LEAD = 12


def chunks_after(gap):
    if gap < 0:
        return range(0, LEAD)
    n = 4 * PHASES
    return range(LEAD + gap * (CHUNKS - LEAD) // n, LEAD + (gap + 1) * (CHUNKS - LEAD) // n)


def size_of(k):
    return SH_SIZES[k] if k < SHT else P


B_ACC, B_UP, B_GATE, B_SCORE, B_TRANS, B_OUT = 0, 2, 3, 4, 6, 7
CREDIT = 2


def build(nc, x, wq, wk, wv, wo, lq1, lk1, lq2, lk2, g, gate_w, bias, w1, w2, w3, sw1, sw2, sw3, out):
    ctx = ExitStack()
    with ctx:
        def sb(name, shape, dt=F32):
            return ctx.enter_context(nc.sbuf_tensor(name, shape, dt))

        def sem(name):
            return ctx.enter_context(nc.semaphore(name))

        qk_parts = nc.dram_tensor("qk_parts", [2, 3, E, T], BF16, kind="Internal").ap()

        xn_hi = sb("xn_hi", [P, KH, T], F32R)
        xn_lo = sb("xn_lo", [P, KH, T], F32R)
        w13 = sb("w13", [P, 2 * KH, ROUTED + SHARED])
        w2r = sb("w2r", [P, UNITS, E])
        wraw = sb("wraw", [P, 4, KH, E])
        w_ring = sb("w_ring", [P, 2, 2, 2 * KH, P], F32R)
        w2_ring = sb("w2_ring", [P, 2, 2, E], F32R)
        v_all = sb("v_all", [P, NT, E])
        v_hi = sb("v_hi", [P, NT, P], F32R)
        v_lo = sb("v_lo", [P, NT, P], F32R)
        cwb = sb("cwb", [P, T])
        cw_half = sb("cw_half", [P, TH])
        qs = sb("qs", [P, 2, 2, T], BF16)
        ks = sb("ks", [P, 2, 2, T], BF16)
        probs = sb("probs", [P, 2, 2, T])
        at_hi = sb("at_hi", [P, 2, BANK], F32R)
        at_lo = sb("at_lo", [P, 2, BANK], F32R)
        hid = sb("hid", [P, 2, TH])
        h_hi = sb("h_hi", [P, 2, TH], F32R)
        h_lo = sb("h_lo", [P, 2, TH], F32R)
        ot = sb("ot", [P, HALVES, T])
        gate = sb("gate", [P, NT, E])
        ident = sb("ident", [P, P])
        ident_bf = sb("ident_bf", [P, P], BF16)
        causal = sb("causal", [P, P], BF16)
        lower16 = sb("lower16", [P, EXPERTS, EXPERTS])
        negmax = sb("negmax", [P, 4, 2])
        coef = sb("coef", [P, 4, 2])
        sums = sb("sums", [P, 2, HALVES, STEPS])
        gcol = sb("gcol", [P, 2])
        gw_raw = sb("gw_raw", [EXPERTS, E])
        gwt = sb("gwt", [P, 2, KH, EXPERTS], F32R)
        bias_b = sb("bias_b", [P, EXPERTS])
        lams = sb("lams", [P, 4, D])
        lam_t = sb("lam_t", [P, 8])
        stats = sb("stats", [P, NT, 6])
        mv = sb("mv", [P, NT, 2])
        ln_t = sb("ln_t", [P, 4, NT])

        ps = ctx.enter_context(nc.psum_tensor("ps", [P, 8 * BANK], F32))

        def bank(b, n=1, rows=P):
            return ps[0:rows, b * BANK:(b + n) * BANK]

        small = wraw[:, 0:2].rearrange("p n k e -> p (n k e)").rearrange("p (n t) -> p n t", n=8)
        xt = probs[:, 0].rearrange("p c (i e) -> p (c i) e", e=E)
        rank_a = probs[:, 1, 0].bitcast(BF16)
        rank_b = probs[:, 1, 1].bitcast(BF16)
        cw_rep = probs[:, 0, 0].rearrange("p (i r) -> p i r", r=P)
        resid = cwb[:, :].rearrange("p (s n) -> p s n", n=BANK)
        lg_t = hid[:, 0]
        stage = [t[:, :, :].rearrange("p a b -> p (a b)").bitcast(BF16)[:, 0:3 * T].rearrange("p (a t) -> p a t", a=3)
                 for t in (ot, gate)]
        sel_g = small[:, 0, 0:NT * GROUPS].rearrange("p (i a) -> p i a", a=GROUPS)

        def table(n):
            return small[:, n].rearrange("p (i e) -> p i e", e=EXPERTS)

        s_x1, s_wqkv, s_gatew, s_vecs, s_sh, s_w13, s_w2, s_wo = map(
            sem, ["x_in", "wqkv_in", "gate_in", "vecs_in", "shared_in", "w13_in", "w2_in", "wo_in"])
        s_x = [s_x1, sem("x_in_2")]
        s_const = sem("const_made")
        s_link_v, s_link_p, s_link_a = sem("vector_link"), sem("pool_link"), sem("scalar_link")
        s_var, s_std, s_xn, s_xt, s_xhi, s_xlo = map(
            sem, ["var_ready", "std_ready", "xn_ready", "xn_transposed", "xn_hi_ready", "xn_lo_ready"])
        s_gwt_ps, s_gwt_hi, s_gwt = sem("gate_transposed"), sem("gate_hi_ready"), sem("gate_parts_ready")
        s_phi, s_plo = sem("proj_hi_ready"), sem("proj_lo_ready")
        s_proj, s_part0, s_parts = map(sem, ["proj_done", "part0_ready", "parts_ready"])
        s_stored = [sem(f"parts_stored_{n}") for n in range(4)]
        s_v = sem("v_ready")
        s_lgt, s_lgc, s_lg, s_el, s_cwrep, s_cwt, s_cwb = map(
            sem, ["logits_t_done", "logits_t_copied", "logits_done", "exp_logits_ready", "weights_ready",
                  "weights_transposed", "weights_spread"])
        s_dot, s_edot, s_lam = sem("lambda_dots"), sem("lambda_exps"), sem("lambda_ready")

        s_w13hi, s_w13lo, s_w2hi, s_w2lo = map(sem, ["w13_hi_split", "w13_lo_split", "w2_hi_split", "w2_lo_split"])
        s_a, s_b, s_th, s_u, s_uc, s_h, s_hhi, s_hlo, s_down = map(
            sem, ["w1_product", "w3_product", "tanh_ready", "silu_ready", "weighted_ready", "hidden_ready",
                  "hidden_hi", "hidden_lo", "down_done"])
        s_accth, s_accfree = sem("acc_tanh"), sem("acc_free")
        s_stack = [sem(f"stacks_in_{n}") for n in range(2)]
        s_score, s_negmax, s_prob, s_chain, s_comb = map(
            sem, ["scores_done", "negmax_ready", "probs_ready", "coef_chain", "combined"])
        s_trans, s_athi, s_atlo, s_pv, s_oev = map(
            sem, ["transposed", "trans_hi", "trans_lo", "pv_done", "out_copied"])
        s_vhi, s_vlo = sem("v_hi_split"), sem("v_lo_split")
        s_cwhalf = sem("weights_of_half")
        s_xre, s_sq, s_ss, s_fac, s_sdf, s_frep, s_fps, s_on, s_onhi, s_onlo, s_wohi, s_wolo, s_so, s_res, s_out = map(
            sem, ["x_again", "squares", "sum_squares", "var_of_heads", "std_of_heads", "factors", "factors_t",
                  "normed", "normed_hi", "normed_lo", "wo_hi", "wo_lo", "attn_out", "result", "stored"])

        tail = w13[:, :, :].rearrange("p a b -> p (a b)")
        x_again = tail[:, 0:NT * E].rearrange("p (i e) -> p i e", e=E)
        squares = tail[:, 2048:4096].rearrange("p (a t) -> p a t", a=HALVES)
        frep = tail[:, 4096:6144].rearrange("p (i h r) -> p i h r", h=HEADS, r=DV)
        normed = tail[:, 6144:8192].rearrange("p (a t) -> p a t", a=HALVES)
        result = tail[:, 8192:10240].rearrange("p (i e) -> p i e", e=E)
        fac = tail[:, 10240:10240 + 4 * NT * HEADS].rearrange("p (n a h i) -> p n a h i", n=4, a=HALVES, i=NT)
        head_ones = tail[:, 10496:10500]

        def three(pe_out, a_hi, a_lo, b_hi, b_lo, first, last, skip=False):
            nc.tensor.matmul(pe_out, a_hi, b_hi, start=first, stop=False, skip_group_check=skip)
            nc.tensor.matmul(pe_out, a_hi, b_lo, start=False, stop=False, skip_group_check=skip)
            return nc.tensor.matmul(pe_out, a_lo, b_hi, start=False, stop=last, skip_group_check=skip)

        def proj_w(slot, part, kh):
            return w_ring[:, slot, part].rearrange("p m n -> p (m n)")[:, kh * E:(kh + 1) * E]

        def raw_tile(k):
            if k < SHT:
                return w13[:, :, ROUTED + k * P:ROUTED + k * P + size_of(k)]
            return w13[:, :, 0:ROUTED].rearrange("p m (e h) -> p m e h", h=INTER)[:, :, :, (k - SHT) * Q:(k - SHT + 1) * Q]

        def ring_tile(k, part, dt=None):
            t = w_ring[:, k % 2, part, :, 0:size_of(k)]
            t = t if dt is None else t.bitcast(dt)
            return t if k < SHT else t.rearrange("p m (e q) -> p m e q", q=Q)

        def w2_index(k):
            return k

        block = ctx.enter_context(nc.Block())

        @block.sync
        def _(sp):
            xv = x.rearrange("o (i p) e -> p (o i) e", p=P)
            for half in range(2):
                sp.dma_start(xt[:, half * 4:half * 4 + 4], xv[:, half * 4:half * 4 + 4]).then_inc(s_x[half], 16)
            sp.dma_start(gw_raw[:, :], gate_w).then_inc(s_gatew, 16)
            for n, w in enumerate((wq, wk, wv)):
                sp.dma_start(wraw[:, n], w.rearrange("(k p) e -> p k e", p=P)).then_inc(s_wqkv, 16)
            for n, v in enumerate((lq1, lk1, lq2, lk2)):
                sp.dma_start(lams[:, n], v.rearrange("(o d) -> o d", o=1).to_broadcast([P, D])).then_inc(s_vecs, 16)
            sp.dma_start(bias_b[:, :], bias.rearrange("(o d) -> o d", o=1).to_broadcast([P, EXPERTS])).then_inc(s_vecs, 16)
            for n in range(HH):
                sp.dma_start(gcol[n * DV:(n + 1) * DV, 0:1], g.rearrange("(d o) -> d o", o=1)).then_inc(s_vecs, 16)
            for m, w in enumerate((sw1, sw3)):
                sp.dma_start(w13[:, m * KH:(m + 1) * KH, ROUTED:], w.rearrange("(k p) h -> p k h", p=P)).then_inc(s_sh, 16)
            sp.dma_start(w2r[:, 0:2, :], sw2[0:2 * P].rearrange("(s p) e -> p s e", p=P)).then_inc(s_sh, 16)
            sp.dma_start(w2r[0:SH_SIZES[2], 2, :], sw2[2 * P:]).then_inc(s_sh, 16)
            for m, w in enumerate((w1, w3)):
                for kh in range(KH):
                    sp.dma_start(w13[:, m * KH + kh, 0:ROUTED].rearrange("p (e h) -> p e h", h=INTER),
                                 w[:, kh * P:(kh + 1) * P, :].rearrange("e p h -> p e h")).then_inc(s_w13, 16)
            for e in range(EXPERTS):
                sp.dma_start(w2r[e * Q:(e + 1) * Q, SHT:, :], w2[e].rearrange("(j q) d -> q j d", q=Q)).then_inc(s_w2, 16)
            sp.dma_start(wraw[:, 3], wo.rearrange("(k p) e -> p k e", p=P)).then_inc(s_wo, 16)
            for n in range(4):
                sp.wait_ge(s_parts, 2 * n + 2)
                sp.dma_start(qk_parts[n // 2, :, (n % 2) * P:(n % 2 + 1) * P, :].rearrange("a p t -> p a t"),
                             stage[n % 2]).then_inc(s_stored[n], 16)
            for n in range(4):
                sp.wait_ge(s_stored[n], 16)
            rows = qk_parts.rearrange("s a (f h c d) t -> (s a f h) d c t", f=HALVES, h=HH, c=2)
            with sp.Fori(0, HALVES) as hf:
                for a in range(HH):
                    sp.wait_ge(s_score, hf * (2 * STEPS) + (2 * NT * (a - 1) + CREDIT + 2 * NT))
                    for n in range(2):
                        stack = (qs, ks)[n]
                        for r, part in enumerate((Q_PART, K_PART)[n]):
                            row = ((n * 3 + part) * HALVES) * HH + a
                            sp.dma_start(stack[r * D:(r + 1) * D, a % 2],
                                         rows[bass.ds(hf * HH + row, 1)].rearrange("o d c t -> (o d) c t")).then_inc(s_stack[a % 2], 16)
            sp.wait_ge(s_fps, 1)
            sp.dma_start(x_again, xv).then_inc(s_xre, 16)
            for i in range(NT):
                sp.wait_ge(s_res, i + 1)
                sp.dma_start(out.rearrange("o (i p) e -> p (o i) e", p=P)[:, i], result[:, i]).then_inc(s_out, 16)
            sp.wait_ge(s_out, 16 * NT)

        @block.tensor
        def _(pe):
            pe.sem_inc(s_a, CREDIT)
            pe.sem_inc(s_b, CREDIT)
            pe.sem_inc(s_down, CREDIT)
            pe.sem_inc(s_trans, 1)
            pe.sem_inc(s_pv, CREDIT)
            pe.sem_inc(s_score, CREDIT + 2 * NT)
            pe.wait_ge(s_const, 1)
            pe.wait_ge(s_gatew, 16)
            for kh in range(KH):
                last = nc.tensor.transpose(ps[:, 3 * BANK + kh * EXPERTS:3 * BANK + (kh + 1) * EXPERTS],
                                           gw_raw[:, kh * P:(kh + 1) * P], ident[0:EXPERTS, 0:EXPERTS])
            last.then_inc(s_gwt_ps, 1)
            for i in range(NT):
                pe.wait_ge(s_xn, i + 1)
                for kh in range(KH):
                    b = 4 + 2 * (i // 4) + kh
                    last = nc.tensor.transpose(ps[:, b * BANK + (i % 4) * P:b * BANK + (i % 4 + 1) * P],
                                               xt[:, i, kh * P:(kh + 1) * P], ident[:, :])
                last.then_inc(s_xt, 1)
            for r in range(8):
                n, mt, c = r // 4, (r // 2) % 2, r % 2
                if r == 0:
                    pe.wait_ge(s_xhi, 4)
                    pe.wait_ge(s_xlo, 4)
                if r % 4 == 0:
                    pe.wait_ge(s_phi, n + 1)
                    pe.wait_ge(s_plo, n + 1)
                if r == 3:
                    pe.wait_ge(s_gwt, 1)
                if r >= 4:
                    pe.wait_ge(s_parts, r - 3)
                for kh in range(KH):
                    last = three(bank(r % 4), proj_w(n, 0, kh)[:, mt * P:(mt + 1) * P], proj_w(n, 1, kh)[:, mt * P:(mt + 1) * P],
                                 xn_hi[:, kh, c * TH:(c + 1) * TH], xn_lo[:, kh, c * TH:(c + 1) * TH], kh == 0, kh == KH - 1)
                last.then_inc(s_proj, 1)
            pe.wait_ge(s_gwt, 1)
            for c in range(2):
                for kh in range(KH):
                    last = three(bank(4 + c, rows=EXPERTS), gwt[:, 0, kh], gwt[:, 1, kh],
                                 xn_hi[:, kh, c * TH:(c + 1) * TH], xn_lo[:, kh, c * TH:(c + 1) * TH], kh == 0, kh == KH - 1)
                last.then_inc(s_lgt, 1)
            for i in range(NT):
                if i % 4 == 0:
                    pe.wait_ge(s_lgc, i // 4 + 1)
                at = (6 + i // 4) * BANK + (i % 4) * EXPERTS
                last = nc.tensor.transpose(ps[:, at:at + EXPERTS],
                                           lg_t[32 * (i // 4):32 * (i // 4) + EXPERTS, (i % 4) * P:(i % 4 + 1) * P],
                                           ident[32 * (i // 4):32 * (i // 4) + EXPERTS, 32 * (i // 4):32 * (i // 4) + EXPERTS])
            last.then_inc(s_lg, 1)
            for r in range(8, 12):
                if r == 8:
                    pe.wait_ge(s_phi, 3)
                    pe.wait_ge(s_plo, 3)
                pe.wait_ge(s_parts, r - 3)
                for i in (2 * (r - 8), 2 * (r - 8) + 1):
                    for kh in range(KH):
                        last = three(ps[:, (r % 4) * BANK + (i % 2) * E:(r % 4) * BANK + (i % 2 + 1) * E],
                                     xn_hi[:, kh, i * P:(i + 1) * P], xn_lo[:, kh, i * P:(i + 1) * P],
                                     proj_w(0, 0, kh), proj_w(0, 1, kh), kh == 0, kh == KH - 1)
                last.then_inc(s_proj, 1)
            pe.wait_ge(s_cwrep, 1)
            for i in range(NT):
                last = nc.tensor.transpose(ps[:, 4 * BANK + i * P:4 * BANK + (i + 1) * P], cw_rep[:, i], ident[:, :])
            last.then_inc(s_cwt, 1)
            pe.wait_ge(s_v, 4)
            pe.wait_ge(s_cwb, 1)
            pe.wait_ge(s_el, 1)

            with pe.Fori(0, HALVES) as hf:
                u0 = hf * UNITS
                n0 = hf * STEPS

                def piece(q):
                    k, r = divmod(q, PIECES)
                    if r < 2:
                        if k == UNITS:
                            return
                        m = size_of(k)
                        if r == 0:
                            pe.wait_ge(s_w13hi, u0 + (k + 1 + CREDIT))
                            pe.wait_ge(s_w13lo, u0 + (k + 1 + CREDIT))
                            pe.wait_ge(s_u, u0 + (k + CREDIT))
                        else:
                            pe.wait_ge(s_h, u0 + (k + CREDIT))
                        for kh in range(KH):
                            last = three(bank(B_UP + r, rows=m), w_ring[:, k % 2, 0, r * KH + kh, 0:m],
                                         w_ring[:, k % 2, 1, r * KH + kh, 0:m], xn_hi[:, kh, bass.ds(hf * TH, TH)],
                                         xn_lo[:, kh, bass.ds(hf * TH, TH)], kh == 0, kh == KH - 1)
                        last.then_inc((s_a, s_b)[r], 1)
                        return
                    k, i, m = k - 1, r - 2, size_of(k - 1)
                    if k < 0:
                        return
                    if i == 0:
                        pe.wait_ge(s_hhi, u0 + (k + 1 + CREDIT))
                        pe.wait_ge(s_hlo, u0 + (k + 1 + CREDIT))
                        pe.wait_ge(s_w2hi, u0 + (k + 1 + CREDIT))
                        pe.wait_ge(s_w2lo, u0 + (k + 1 + CREDIT))
                        if k == 0:
                            pe.wait_ge(s_accfree, hf + 1)
                    at = B_ACC * BANK + i * E
                    last = three(ps[:, at:at + E], h_hi[0:m, k % 2, i * P:(i + 1) * P], h_lo[0:m, k % 2, i * P:(i + 1) * P],
                                 w2_ring[0:m, k % 2, 0], w2_ring[0:m, k % 2, 1], k == 0 and i % 2 == 0, k == UNITS - 1, skip=True)
                    if i == 3:
                        last.then_inc(s_down, 1)

                def scores(s, c):
                    a, i = s // NT, ORDER[s % NT]
                    if c == 0 and s % NT == 0:
                        pe.wait_ge(s_stack[a % 2], hf * (HH // 2 * STACK_DMAS) + STACK_DMAS * (a // 2 + 1))
                    behind = 1 if (i < 4 and c == 1) else 0
                    pe.wait_ge(s_prob, n0 * 2 + (2 * s + c - behind + CREDIT))
                    w = (i + 1) * P
                    q = qs[0:STACK, a % 2, c, i * P:(i + 1) * P]
                    at = (B_SCORE + (c if i < 4 else 0)) * BANK
                    for lo in range(0, w, BANK):
                        hi = min(lo + BANK, w)
                        diagonal = hi == w
                        nc.tensor.matmul(ps[:, at + lo:at + hi], q, ks[0:STACK, a % 2, c, lo:hi], start=True, stop=not diagonal)
                        if diagonal:
                            last = nc.tensor.matmul(ps[:, at + w - P:at + w], ident_bf[:, :], causal[:, :], start=False, stop=True)
                    last.then_inc(s_score, 1)

                def transposes(s, grp):
                    if not 0 <= s < STEPS or grp >= GROUP_OF[s]:
                        return
                    i = ORDER[s % NT]
                    gi = FIRST_GROUP[s] + grp
                    if grp == 0:
                        pe.wait_ge(s_comb, n0 + (s + 1 + CREDIT))
                    pe.wait_ge(s_atlo, hf * GPH + (gi + CREDIT))
                    for j in range(4 * grp, min(4 * grp + 4, i + 1)):
                        last = nc.tensor.transpose(ps[:, B_TRANS * BANK + (j % 4) * P:B_TRANS * BANK + (j % 4 + 1) * P],
                                                   probs[:, s % 2, 0, j * P:(j + 1) * P], ident[:, :])
                    last.then_inc(s_trans, 1)

                def values(s, grp):
                    if not 0 <= s < STEPS or grp >= GROUP_OF[s]:
                        return
                    a, i = s // NT, ORDER[s % NT]
                    gi = FIRST_GROUP[s] + grp
                    if s == 0 and grp == 0:
                        pe.wait_ge(s_vhi, hf + 1)
                        pe.wait_ge(s_vlo, hf + 1)
                    if grp == 0:
                        pe.wait_ge(s_oev, n0 + (s + CREDIT))
                    pe.wait_ge(s_athi, hf * GPH + (gi + 1 + CREDIT))
                    pe.wait_ge(s_atlo, hf * GPH + (gi + 1 + CREDIT))
                    for j in range(4 * grp, min(4 * grp + 4, i + 1)):
                        last = three(ps[0:DV, B_OUT * BANK:B_OUT * BANK + P], v_hi[:, j, a * DV:(a + 1) * DV], v_lo[:, j, a * DV:(a + 1) * DV],
                                     at_hi[:, gi % 2, (j % 4) * P:(j % 4 + 1) * P], at_lo[:, gi % 2, (j % 4) * P:(j % 4 + 1) * P],
                                     j == 0, j == i)
                    last.then_inc(s_pv, 1)

                for gap in range(-1, 4 * PHASES):
                    p, sub = divmod(gap, 4)
                    if gap >= 0 and sub == 0:
                        if p < STEPS:
                            scores(p, 0)
                        values(p - 2, 0)
                    if gap >= 0 and sub == 1:
                        transposes(p - 1, 0)
                    if gap >= 0 and sub == 2:
                        if p < STEPS:
                            scores(p, 1)
                        values(p - 2, 1)
                    if gap >= 0 and sub == 3:
                        transposes(p - 1, 1)
                    for q in chunks_after(gap):
                        piece(q)

            pe.wait_ge(s_sq, 1)
            for hf in range(HALVES):
                for i in range(NT):
                    at = (4 + hf) * BANK + i * HH
                    last = nc.tensor.matmul(ps[:, at:at + HH], squares[:, hf, i * P:(i + 1) * P], head_ones, start=True, stop=True)
            last.then_inc(s_ss, 1)
            pe.wait_ge(s_frep, 1)
            pe.wait_ge(s_accfree, 3)
            for hf in range(HALVES):
                for i in range(NT):
                    at = 2 * hf * BANK + i * P
                    last = nc.tensor.transpose(ps[:, at:at + P], frep[:, i, hf * HH:(hf + 1) * HH].rearrange("p h r -> p (h r)"), ident[:, :])
            last.then_inc(s_fps, 1)
            pe.wait_ge(s_wohi, 1)
            pe.wait_ge(s_wolo, 1)
            pe.wait_ge(s_onhi, 2)
            pe.wait_ge(s_onlo, 2)
            for i in range(NT):
                b = 4 + i // 2
                for kh in range(KH):
                    last = three(ps[:, b * BANK + (i % 2) * E:b * BANK + (i % 2 + 1) * E],
                                 xn_hi[:, kh, i * P:(i + 1) * P], xn_lo[:, kh, i * P:(i + 1) * P],
                                 proj_w(1, 0, kh), proj_w(1, 1, kh), kh == 0, kh == KH - 1)
                if i % 2 == 1:
                    last.then_inc(s_so, 1)

        @block.scalar
        def _(act):
            for s in (s_w13hi, s_w2hi, s_th, s_hhi, s_prob, s_athi, s_oev):
                act.sem_inc(s, CREDIT)

            def split_hi(n):
                slot = (0, 1, 0, 1)[n]
                return nc.scalar.activation(w_ring[:, slot, 0].rearrange("p m n -> p (m n)"),
                                            wraw[:, n].rearrange("p k e -> p (k e)"), ACT.Copy)

            act.wait_ge(s_gwt_ps, 1)
            nc.scalar.activation(gwt[:, 0].rearrange("p k e -> p (k e)"), ps[:, 3 * BANK:3 * BANK + KH * EXPERTS], ACT.Copy).then_inc(s_gwt_hi, 1)
            act.wait_ge(s_wqkv, 48)
            split_hi(0).then_inc(s_phi, 1)
            split_hi(1).then_inc(s_phi, 1)
            act.wait_ge(s_var, 1)
            nc.scalar.activation(ln_t[:, 1], ln_t[:, 0], ACT.Sqrt).then_inc(s_std, 1)
            act.wait_ge(s_dot, 1)
            nc.scalar.activation(lam_t[:, 2:4], lam_t[:, 0:2], ACT.Exp).then_inc(s_edot, 1)
            for c in range(2):
                act.wait_ge(s_xt, 4 * c + 4)
                for kh in range(KH):
                    nc.scalar.activation(xn_hi[:, kh, c * TH:(c + 1) * TH], bank(4 + 2 * c + kh), ACT.Copy).then_inc(s_xhi, 1)
            for r in range(8):
                n, c = r // 4, r % 2
                act.wait_ge(s_proj, r + 1)
                if r >= 4 and c == 0:
                    act.wait_ge(s_stored[r // 2 - 2], 16)
                nc.scalar.activation(stage[(r // 2) % 2][:, 0, c * TH:(c + 1) * TH], bank(r % 4), ACT.Copy,
                                     scale=D ** -0.5 if n == 0 else 1.0).then_inc(s_part0, 1)
                if r == 3:
                    act.wait_ge(s_plo, 1)
                    split_hi(2).then_inc(s_phi, 1)
            for c in range(2):
                act.wait_ge(s_lgt, c + 1)
                nc.scalar.activation(lg_t[32 * c:32 * c + EXPERTS, :], bank(4 + c, rows=EXPERTS), ACT.Copy).then_inc(s_lgc, 1)
            act.wait_ge(s_lg, 1)
            nc.scalar.activation(small[:, 1].rearrange("p (b n) -> p b n", b=2), bank(6, 2).rearrange("p (b n) -> p b n", b=2)[:, :, 0:4 * EXPERTS],
                                 ACT.Exp, scale=-1.0).then_inc(s_el, 1)
            for r in range(4):
                act.wait_ge(s_proj, 9 + r)
                nc.scalar.activation(v_all[:, 2 * r:2 * r + 2].rearrange("p i e -> p (i e)"), bank(r % 4), ACT.Copy).then_inc(s_v, 1)
            act.wait_ge(s_cwt, 1)
            nc.scalar.activation(cwb[:, :], bank(4, 2), ACT.Copy).then_inc(s_cwb, 1)
            act.wait_ge(s_v, 4)
            act.wait_ge(s_cwb, 1)

            with act.Fori(0, HALVES) as hf:
                u0 = hf * UNITS
                n0 = hf * STEPS

                def split_w13(k):
                    act.wait_ge(s_b, u0 + (k + 1))
                    nc.scalar.activation(ring_tile(k, 0), raw_tile(k), ACT.Copy).then_inc(s_w13hi, 1)

                def split_w2(k):
                    m = size_of(k)
                    act.wait_ge(s_down, u0 + (k + 1))
                    nc.scalar.activation(w2_ring[0:m, k % 2, 0], w2r[0:m, w2_index(k)], ACT.Copy).then_inc(s_w2hi, 1)

                def high_hidden(k):
                    if k < 0:
                        return
                    m = size_of(k)
                    act.wait_ge(s_h, u0 + (k + 1 + CREDIT))
                    act.wait_ge(s_down, u0 + (k + 1))
                    nc.scalar.activation(h_hi[0:m, k % 2], hid[0:m, k % 2], ACT.Copy).then_inc(s_hhi, 1)

                def piece(q):
                    k, r = divmod(q, PIECES)
                    if r == 0:
                        high_hidden(k - 1)
                    if k == UNITS:
                        return
                    m = size_of(k)
                    if r == 1:
                        act.wait_ge(s_a, u0 + (k + 1 + CREDIT))
                        act.wait_ge(s_hlo, u0 + (k - 1 + CREDIT))
                        nc.scalar.activation(hid[0:m, k % 2], bank(B_UP, rows=m), ACT.Tanh, scale=0.5).then_inc(s_th, 1)
                    elif r == 3:
                        split_w2(k)
                    elif r == 4 and k + 2 < UNITS:
                        split_w13(k + 2)

                def exponentials(s, c):
                    i = ORDER[s % NT]
                    w = (i + 1) * P
                    at = (B_SCORE + (c if i < 4 else 0)) * BANK
                    act.wait_ge(s_negmax, n0 * 2 + (2 * s + c + 1))
                    if c == 0:
                        act.wait_ge(s_trans, hf * GPH + (FIRST_GROUP[s - 1] + 1 if s else 1 - 0))
                    nc.scalar.activation(probs[:, s % 2, c, 0:w], ps[:, at:at + w], ACT.Exp, bias=negmax[:, s % 4, c:c + 1],
                                         accum_out=sums[:, c, bass.ds(hf, 1), s]).then_inc(s_prob, 1)

                def copy_trans(s, grp):
                    if not 0 <= s < STEPS or grp >= GROUP_OF[s]:
                        return
                    gi = FIRST_GROUP[s] + grp
                    w = min(BANK, (ORDER[s % NT] + 1 - 4 * grp) * P)
                    act.wait_ge(s_trans, hf * GPH + (gi + 2))
                    act.wait_ge(s_pv, hf * GPH + (gi + 1))
                    nc.scalar.activation(at_hi[:, gi % 2, 0:w], ps[:, B_TRANS * BANK:B_TRANS * BANK + w], ACT.Copy).then_inc(s_athi, 1)

                def copy_out(s):
                    if not 0 <= s < STEPS:
                        return
                    a, i = s // NT, ORDER[s % NT]
                    act.wait_ge(s_pv, hf * GPH + (FIRST_GROUP[s] + GROUP_OF[s] + CREDIT))
                    nc.scalar.activation(ot[a * DV:(a + 1) * DV, bass.ds(hf, 1), i * P:(i + 1) * P].rearrange("p o t -> p (o t)"),
                                         ps[0:DV, B_OUT * BANK:B_OUT * BANK + P], ACT.Copy).then_inc(s_oev, 1)

                act.wait_ge(s_pv, hf * GPH + CREDIT)
                nc.scalar.activation(v_hi[:, :, :], v_all[:, :, bass.ds(hf * P, P)], ACT.Copy).then_inc(s_vhi, 1)
                act.wait_ge(s_uc, hf * RTILES + 1)
                nc.scalar.activation(cw_half[:, :], cwb[:, bass.ds(hf * TH, TH)], ACT.Copy).then_inc(s_cwhalf, 1)
                act.wait_ge(s_sh, 64)
                split_w13(0)
                split_w13(1)
                for gap in range(-1, 4 * PHASES):
                    p, sub = divmod(gap, 4)
                    if gap >= 0 and sub == 0:
                        copy_trans(p - 2, 1)
                        if p < STEPS:
                            exponentials(p, 0)
                    if gap >= 0 and sub == 2:
                        copy_trans(p - 1, 0)
                        if p < STEPS:
                            exponentials(p, 1)
                    if gap >= 0 and sub == 3:
                        copy_out(p - 2)
                    for q in chunks_after(gap):
                        if q == PIECES * (SHT - 2) + 4:
                            act.wait_ge(s_w13, 64)
                            act.wait_ge(s_w2, 256)
                        piece(q)
                act.wait_ge(s_down, u0 + (UNITS + CREDIT))
                act.wait_ge(s_trans, hf * GPH + (GPH + 1))
                nc.scalar.activation(probs[:, 0, 0], bank(B_ACC, 2), ACT.Tanh, scale=0.5).then_inc(s_accth, 1)

            act.wait_ge(s_oev, HALVES * STEPS + CREDIT)
            act.wait_ge(s_fac, 1)
            nc.scalar.activation(squares[:, :, :], ot[:, :, :], ACT.Square).then_inc(s_sq, 1)
            act.wait_ge(s_wo, 16)
            act.wait_ge(s_b, HALVES * UNITS + CREDIT)
            split_hi(3).then_inc(s_wohi, 1)
            act.wait_ge(s_fac, 2)
            nc.scalar.activation(fac[:, 2], fac[:, 1], ACT.Sqrt).then_inc(s_sdf, 1)
            for hf in range(HALVES):
                act.wait_ge(s_on, hf + 1)
                nc.scalar.activation(xn_hi[:, hf], normed[:, hf], ACT.Copy).then_inc(s_onhi, 1)

        @block.vector
        def _(dve):
            links = [0]

            def link(ins):
                links[0] += 1
                ins.then_inc(s_link_v, 1)
                dve.wait_ge(s_link_v, links[0])

            for s in (s_u, s_h, s_comb, s_atlo):
                dve.sem_inc(s, CREDIT)
            dve.sem_inc(s_accfree, 1)
            for i in range(NT):
                if i % 4 == 0:
                    dve.wait_ge(s_x[i // 4], 16)
                last = nc.vector.bn_stats(stats[:, i], xt[:, i])
            link(last)
            for i in range(NT):
                last = nc.vector.bn_aggr(mv[:, i], stats[:, i])
            link(last)
            nc.vector.tensor_scalar(ln_t[:, 0], mv[:, :, 1], EPS, None, ALU.add).then_inc(s_var, 1)
            dve.wait_ge(s_std, 1)
            link(nc.vector.reciprocal(ln_t[:, 1], ln_t[:, 1]))
            link(nc.vector.tensor_tensor(ln_t[:, 2], ln_t[:, 1], ln_t[:, 1], ALU.mult))
            link(nc.vector.tensor_tensor(ln_t[:, 2], ln_t[:, 2], ln_t[:, 0], ALU.mult))
            link(nc.vector.tensor_scalar(ln_t[:, 2], ln_t[:, 2], -0.5, 1.5, ALU.mult, ALU.add))
            link(nc.vector.tensor_tensor(ln_t[:, 1], ln_t[:, 1], ln_t[:, 2], ALU.mult))
            for i in range(NT):
                nc.vector.tensor_scalar(xt[:, i], xt[:, i], mv[:, i, 0:1], ln_t[:, 1, i:i + 1], ALU.subtract, ALU.mult).then_inc(s_xn, 1)
            dve.wait_ge(s_vecs, 144)
            for n in range(2):
                link(nc.vector.tensor_tensor(lams[:, 2 * n], lams[:, 2 * n], lams[:, 2 * n + 1], ALU.mult))
                last = nc.vector.tensor_reduce(lam_t[:, n:n + 1], lams[:, 2 * n], axis=X, op=ALU.add)
            last.then_inc(s_dot, 1)
            dve.wait_ge(s_edot, 1)
            nc.vector.scalar_tensor_tensor(lam_t[:, 4:5], lam_t[:, 3:4], -LAMBDA_INIT, lam_t[:, 2:3], ALU.add, ALU.subtract).then_inc(s_lam, 1)
            nc.vector.tensor_scalar(gcol[:, 1:2], gcol[:, 0:1], 1.0 - LAMBDA_INIT, None, ALU.mult).then_inc(s_lam, 1)
            dve.wait_ge(s_gwt_hi, 1)
            nc.vector.tensor_tensor(gwt[:, 1].rearrange("p k e -> p (k e)"), ps[:, 3 * BANK:3 * BANK + KH * EXPERTS],
                                    gwt[:, 0].bitcast(F32).rearrange("p k e -> p (k e)"), ALU.subtract).then_inc(s_gwt, 1)
            for r in range(4):
                c, kh = r // 2, r % 2
                dve.wait_ge(s_xhi, r + 1)
                nc.vector.tensor_tensor(xn_lo[:, kh, c * TH:(c + 1) * TH], bank(4 + r),
                                        xn_hi[:, kh, c * TH:(c + 1) * TH].bitcast(F32), ALU.subtract).then_inc(s_xlo, 1)
            for r in range(8):
                n, c = r // 4, r % 2
                st = stage[(r // 2) % 2]
                at = slice(c * TH, (c + 1) * TH)
                dve.wait_ge(s_part0, r + 1)
                link(nc.vector.scalar_tensor_tensor(resid[:, r % 2], bank(r % 4), D ** -0.5 if n == 0 else 1.0, st[:, 0, at], ALU.mult, ALU.subtract))
                link(nc.vector.tensor_copy(st[:, 1, at], resid[:, r % 2]))
                nc.vector.tensor_tensor(st[:, 2, at], resid[:, r % 2], st[:, 1, at], ALU.subtract).then_inc(s_parts, 1)

            sig, sc, masked, sel = table(2), table(3), table(4), table(5)
            dve.wait_ge(s_el, 1)
            link(nc.vector.tensor_scalar(small[:, 1], small[:, 1], 1.0, None, ALU.add))
            link(nc.vector.reciprocal(small[:, 2], small[:, 1]))
            link(nc.vector.tensor_tensor(sc, sig, bias_b[:, :].rearrange("p (o e) -> p o e", o=1).to_broadcast([P, NT, EXPERTS]), ALU.add))
            gmax = small[:, 6, 0:NT * GROUPS].rearrange("p (i a) -> p i a", a=GROUPS)
            link(nc.vector.tensor_reduce(gmax, small[:, 3].rearrange("p (i a e) -> p i a e", a=GROUPS, e=PER_GROUP), axis=X, op=ALU.max))

            dve.wait_ge(s_const, 2)

            def rank(out, values, n, tmp_a, tmp_b, tile0, tiles):
                shape = [P, tiles, n, n]
                mine = values[:, tile0:tile0 + tiles].rearrange("p i (e o) -> p i e o", o=1).to_broadcast(shape)
                theirs = values[:, tile0:tile0 + tiles].rearrange("p i (o e) -> p i o e", o=1).to_broadcast(shape)
                lower = lower16[:, 0:n, 0:n].rearrange("p (o e) f -> p o e f", o=1).to_broadcast(shape)
                a = tmp_a[:, 0:tiles * n * n].rearrange("p (i e f) -> p i e f", e=n, f=n)
                b = tmp_b[:, 0:tiles * n * n].rearrange("p (i e f) -> p i e f", e=n, f=n)
                link(nc.vector.tensor_tensor(a, theirs, mine, ALU.is_gt))
                link(nc.vector.tensor_tensor(b, theirs, mine, ALU.is_ge))
                link(nc.vector.tensor_tensor(b, b, lower, ALU.mult))
                link(nc.vector.tensor_tensor(a, a, b, ALU.max))
                link(nc.vector.tensor_reduce(out[:, tile0:tile0 + tiles], a, axis=X, op=ALU.add))

            rank(sel_g, gmax, GROUPS, rank_a, rank_b, 0, NT)
            link(nc.vector.tensor_scalar(small[:, 0, 0:NT * GROUPS], small[:, 0, 0:NT * GROUPS], float(TOPG), None, ALU.is_lt))
            link(nc.vector.tensor_scalar(small[:, 6, 0:NT * GROUPS], small[:, 0, 0:NT * GROUPS], 1.0, BIG, ALU.subtract, ALU.mult))

            def by_expert(t):
                return t.rearrange("p (i a o) -> p (i a) o", a=GROUPS, o=1).to_broadcast([P, NT * GROUPS, PER_GROUP])

            m3 = small[:, 4].rearrange("p (i e) -> p i e", e=PER_GROUP)
            link(nc.vector.tensor_tensor(m3, small[:, 3].rearrange("p (i e) -> p i e", e=PER_GROUP), by_expert(small[:, 0, 0:NT * GROUPS]), ALU.mult))
            link(nc.vector.tensor_tensor(m3, m3, by_expert(small[:, 6, 0:NT * GROUPS]), ALU.add))
            rank(sel, masked, EXPERTS, rank_a, rank_b, 0, NT)
            link(nc.vector.tensor_scalar(small[:, 5], small[:, 5], float(TOPK), None, ALU.is_lt))
            link(nc.vector.tensor_tensor(small[:, 5], small[:, 5], small[:, 2], ALU.mult))
            link(nc.vector.tensor_reduce(small[:, 7, 0:NT], sel, axis=X, op=ALU.add))
            link(nc.vector.reciprocal(small[:, 7, NT:2 * NT], small[:, 7, 0:NT]))
            link(nc.vector.tensor_scalar(small[:, 7, NT:2 * NT], small[:, 7, NT:2 * NT], 0.5, None, ALU.mult))
            link(nc.vector.tensor_tensor(sel, sel, small[:, 7, NT:2 * NT].rearrange("p (i o) -> p i o", o=1).to_broadcast([P, NT, EXPERTS]), ALU.mult))
            nc.vector.tensor_copy(cw_rep.rearrange("p i (e q) -> p (i e) q", q=Q),
                                  small[:, 5].rearrange("p (n o) -> p n o", o=1).to_broadcast([P, NT * EXPERTS, Q])).then_inc(s_cwrep, 1)
            dve.wait_ge(s_lam, 2)

            with dve.Fori(0, HALVES) as hf:
                u0 = hf * UNITS
                n0 = hf * STEPS

                def piece(q):
                    k, r = divmod(q, PIECES)
                    if k == UNITS:
                        return
                    m = size_of(k)
                    if r == 2:
                        dve.wait_ge(s_th, u0 + (k + 1 + CREDIT))
                        nc.vector.scalar_tensor_tensor(hid[0:m, k % 2], hid[0:m, k % 2], 1.0, bank(B_UP, rows=m), ALU.add, ALU.mult).then_inc(s_u, 1)
                    elif r == 5:
                        dve.wait_ge(s_b, u0 + (k + 1 + CREDIT))
                        if k < SHT:
                            dve.wait_ge(s_u, u0 + (k + 1 + CREDIT))
                            nc.vector.scalar_tensor_tensor(hid[0:m, k % 2], hid[0:m, k % 2], 0.5, bank(B_GATE, rows=m), ALU.mult, ALU.mult).then_inc(s_h, 1)
                        else:
                            dve.wait_ge(s_uc, hf * RTILES + (k - SHT + 2))
                            nc.vector.tensor_tensor(hid[0:m, k % 2], hid[0:m, k % 2], bank(B_GATE, rows=m), ALU.mult).then_inc(s_h, 1)

                def maxima(s, c):
                    i = ORDER[s % NT]
                    w = (i + 1) * P
                    at = (B_SCORE + (c if i < 4 else 0)) * BANK
                    dve.wait_ge(s_score, n0 * 2 + (2 * s + c + 1 + CREDIT + 2 * NT))
                    nc.vector.tensor_reduce(negmax[:, s % 4, c:c + 1], ps[:, at:at + w], axis=X, op=ALU.max, negate=True).then_inc(s_negmax, 1)

                def combine(s):
                    if not 0 <= s < STEPS:
                        return
                    w = (ORDER[s % NT] + 1) * P
                    r2, cf = coef[:, s % 4, 0:1], coef[:, s % 4, 1:2]
                    dve.wait_ge(s_prob, n0 * 2 + (2 * s + 2 + CREDIT))
                    nc.vector.reciprocal(r2, sums[:, 1, bass.ds(hf, 1), s]).then_inc(s_chain, 1)
                    dve.wait_ge(s_chain, n0 * 2 + (2 * s + 1))
                    nc.vector.tensor_scalar(cf, r2, sums[:, 0, bass.ds(hf, 1), s], lam_t[:, 4:5], ALU.mult, ALU.mult).then_inc(s_chain, 1)
                    dve.wait_ge(s_chain, n0 * 2 + (2 * s + 2))
                    nc.vector.scalar_tensor_tensor(probs[:, s % 2, 0, 0:w], probs[:, s % 2, 1, 0:w], cf, probs[:, s % 2, 0, 0:w],
                                                   ALU.mult, ALU.add).then_inc(s_comb, 1)

                def copy_trans(s, grp):
                    if not 0 <= s < STEPS or grp >= GROUP_OF[s]:
                        return
                    gi = FIRST_GROUP[s] + grp
                    w = min(BANK, (ORDER[s % NT] + 1 - 4 * grp) * P)
                    dve.wait_ge(s_athi, hf * GPH + (gi + 1 + CREDIT))
                    nc.vector.tensor_tensor(at_lo[:, gi % 2, 0:w], ps[:, B_TRANS * BANK:B_TRANS * BANK + w],
                                            at_hi[:, gi % 2, 0:w].bitcast(F32), ALU.subtract).then_inc(s_atlo, 1)

                dve.wait_ge(s_vhi, hf + 1)
                nc.vector.tensor_tensor(v_lo[:, :, :], v_all[:, :, bass.ds(hf * P, P)], v_hi[:, :, :].bitcast(F32), ALU.subtract).then_inc(s_vlo, 1)
                for gap in range(-1, 4 * PHASES):
                    p, sub = divmod(gap, 4)
                    if gap >= 0 and sub == 0:
                        combine(p - 1)
                        copy_trans(p - 2, 1)
                        if p < STEPS:
                            maxima(p, 0)
                    if gap >= 0 and sub == 2:
                        copy_trans(p - 1, 0)
                        if p < STEPS:
                            maxima(p, 1)
                    for q in chunks_after(gap):
                        piece(q)
                dve.wait_ge(s_accth, hf + 1)
                nc.vector.scalar_tensor_tensor(gate[:, bass.ds(hf * 4, 4)].rearrange("p i e -> p (i e)"), probs[:, 0, 0], 1.0, bank(B_ACC, 2),
                                               ALU.add, ALU.mult).then_inc(s_accfree, 1)

            dve.wait_ge(s_w13lo, HALVES * UNITS + CREDIT)
            dve.wait_ge(s_w13hi, HALVES * UNITS + CREDIT)
            link(nc.vector.memset(head_ones, 0.0))
            for n in range(HH):
                last = nc.vector.memset(tail[n * DV:(n + 1) * DV, 10496 + n:10497 + n], 1.0 / DV)
            last.then_inc(s_fac, 1)
            l1 = sums[:, 0].rearrange("p f (h i) -> p f h i", i=NT)
            link(nc.vector.tensor_tensor(fac[:, 0], l1, l1, ALU.mult))
            dve.wait_ge(s_ss, 1)
            for hf in range(HALVES):
                for pos, i in enumerate(ORDER):
                    src = ps[:, (4 + hf) * BANK + i * HH:(4 + hf) * BANK + (i + 1) * HH]
                    last = nc.vector.scalar_tensor_tensor(fac[:, 1, hf, :, pos], fac[:, 0, hf, :, pos], EPS, src, ALU.mult, ALU.add)
            last.then_inc(s_fac, 1)
            dve.wait_ge(s_sdf, 1)
            link(nc.vector.reciprocal(fac[:, 2], fac[:, 2]))
            link(nc.vector.tensor_tensor(fac[:, 3], fac[:, 2], fac[:, 2], ALU.mult))
            link(nc.vector.tensor_tensor(fac[:, 3], fac[:, 3], fac[:, 1], ALU.mult))
            link(nc.vector.tensor_scalar(fac[:, 3], fac[:, 3], -0.5, 1.5, ALU.mult, ALU.add))
            link(nc.vector.tensor_tensor(fac[:, 2], fac[:, 2], fac[:, 3], ALU.mult))
            for pos, i in enumerate(ORDER):
                last = nc.vector.tensor_copy(frep[:, i], fac[:, 2, :, :, pos].rearrange("p f h -> p (f h)").rearrange("p (h o) -> p h o", o=1)
                                             .to_broadcast([P, HEADS, DV]))
            last.then_inc(s_frep, 1)
            dve.wait_ge(s_fps, 1)
            for hf in range(HALVES):
                nc.vector.scalar_tensor_tensor(normed[:, hf], ot[:, hf], gcol[:, 1:2], bank(2 * hf, 2), ALU.mult, ALU.mult).then_inc(s_on, 1)
            for hf in range(HALVES):
                dve.wait_ge(s_onhi, hf + 1)
                nc.vector.tensor_tensor(xn_lo[:, hf], normed[:, hf], xn_hi[:, hf].bitcast(F32), ALU.subtract).then_inc(s_onlo, 1)
            dve.wait_ge(s_xre, 16)
            for r in range(4):
                two = slice(2 * r, 2 * r + 2)
                dve.wait_ge(s_so, r + 1)
                link(nc.vector.tensor_tensor(result[:, two], gate[:, two], bank(4 + r).rearrange("p (i e) -> p i e", e=E), ALU.mult))
                for i in (2 * r, 2 * r + 1):
                    nc.vector.scalar_tensor_tensor(result[:, i], result[:, i], 0.5, x_again[:, i], ALU.mult, ALU.add).then_inc(s_res, 1)

        @block.gpsimd
        def _(pool):
            links = [0]

            def link(ins):
                links[0] += 1
                ins.then_inc(s_link_p, 1)
                pool.wait_ge(s_link_p, links[0])

            for s in (s_w13lo, s_w2lo, s_hlo):
                pool.sem_inc(s, CREDIT)
            pool.sem_inc(s_uc, 1)
            link(pool.memset(ident[:, :], 0.0))
            pool.affine_select(out=ident[:, :], in_=ident[:, :], compare_op=ALU.not_equal, fill=1.0, base=0,
                               pattern=[[-1, P]], channel_multiplier=1).then_inc(s_const, 1)
            link(pool.memset(lower16[:, :, :], 1.0))
            link(pool.affine_select(out=lower16[:, :, :], in_=lower16[:, :, :], compare_op=ALU.is_ge, fill=0.0, base=-1,
                                    pattern=[[1, EXPERTS], [-1, EXPERTS]], channel_multiplier=0))
            link(pool.memset(ident_bf[:, :], 0.0))
            link(pool.affine_select(out=ident_bf[:, :], in_=ident_bf[:, :], compare_op=ALU.not_equal, fill=1.0, base=0,
                                    pattern=[[-1, P]], channel_multiplier=1))
            link(pool.memset(causal[:, :], 0.0))
            pool.affine_select(out=causal[:, :], in_=causal[:, :], compare_op=ALU.is_ge, fill=-BIG, base=0,
                               pattern=[[-1, P]], channel_multiplier=1).then_inc(s_const, 1)

            def split_lo(n):
                slot = (0, 1, 0, 1)[n]
                return pool.tensor_tensor(out=w_ring[:, slot, 1].rearrange("p m n -> p (m n)"), in0=wraw[:, n].rearrange("p k e -> p (k e)"),
                                          in1=w_ring[:, slot, 0].bitcast(F32).rearrange("p m n -> p (m n)"), op=ALU.subtract)

            for n in range(3):
                pool.wait_ge(s_phi, n + 1)
                if n == 2:
                    pool.wait_ge(s_proj, 4)
                split_lo(n).then_inc(s_plo, 1)
            pool.wait_ge(s_v, 4)
            pool.wait_ge(s_cwb, 1)

            with pool.Fori(0, HALVES) as hf:
                u0 = hf * UNITS

                def split_w13(k):
                    pool.wait_ge(s_w13hi, u0 + (k + 1 + CREDIT))
                    pool.tensor_tensor(out=ring_tile(k, 1), in0=raw_tile(k), in1=ring_tile(k, 0, F32), op=ALU.subtract).then_inc(s_w13lo, 1)

                def split_w2(k):
                    m = size_of(k)
                    pool.wait_ge(s_w2hi, u0 + (k + 1 + CREDIT))
                    pool.tensor_tensor(out=w2_ring[0:m, k % 2, 1], in0=w2r[0:m, w2_index(k)], in1=w2_ring[0:m, k % 2, 0].bitcast(F32),
                                       op=ALU.subtract).then_inc(s_w2lo, 1)

                def piece(q):
                    k, r = divmod(q, PIECES)
                    if r == 0 and k > 0:
                        m = size_of(k - 1)
                        pool.wait_ge(s_hhi, u0 + (k + CREDIT))
                        pool.tensor_tensor(out=h_lo[0:m, (k - 1) % 2], in0=hid[0:m, (k - 1) % 2], in1=h_hi[0:m, (k - 1) % 2].bitcast(F32),
                                           op=ALU.subtract).then_inc(s_hlo, 1)
                    if k == UNITS:
                        return
                    if r == 2 and k >= SHT:
                        if k == SHT:
                            pool.wait_ge(s_cwhalf, hf + 1)
                        pool.wait_ge(s_u, u0 + (k + 1 + CREDIT))
                        pool.tensor_tensor(out=hid[:, k % 2], in0=hid[:, k % 2], in1=cw_half[:, :], op=ALU.mult).then_inc(s_uc, 1)
                    elif r == 3:
                        split_w2(k)
                    elif r == 4 and k + 2 < UNITS:
                        split_w13(k + 2)

                split_w13(0)
                split_w13(1)
                for q in range(CHUNKS):
                    piece(q)
            pool.wait_ge(s_wohi, 1)
            split_lo(3).then_inc(s_wolo, 1)


_INS = ["L0_attn_x", "L0_attn_Wq", "L0_attn_Wk", "L0_attn_Wv", "L0_attn_Wo", "L0_attn_lambda_q1", "L0_attn_lambda_k1",
        "L0_attn_lambda_q2", "L0_attn_lambda_k2", "L0_attn_g", "L0_ffn_gate_w", "L0_ffn_expert_bias", "L0_ffn_w1",
        "L0_ffn_w2", "L0_ffn_w3", "L0_ffn_sw1", "L0_ffn_sw2", "L0_ffn_sw3"]


def kernel(**inputs):
    import numpy as _np
    import concourse.bacc as _bacc
    from concourse.bass_utils import run_bass_kernel_spmd as _run

    nc = _bacc.Bacc("TRN2", target_bir_lowering=False, num_devices=1)
    arrays, args = {}, []
    for name in _INS:
        a = _np.ascontiguousarray(inputs[name])
        arrays[name] = a
        args.append(nc.dram_tensor(name, a.shape, mybir.dt.from_np(a.dtype), kind="ExternalInput").ap())
    out = nc.dram_tensor("out", (1, T, E), F32, kind="ExternalOutput").ap()
    build(nc, *args, out)
    r = _run(nc, [arrays], core_ids=[0])
    return r.results[0]["out"]
```

```python
import math
from contextlib import ExitStack

import numpy as np

import concourse.bass as bass
from concourse import mybir

F32 = mybir.dt.float32
F32R = mybir.dt.float32r
BF16 = mybir.dt.bfloat16
ALU = mybir.AluOpType
ACT = mybir.ActivationFunctionType
X = mybir.AxisListType.X

P = 128
BANK = 512
T = 1024
E = 256
NT = T // P
KH = E // P
HEADS = 8
D = 16
DV = 2 * D
HALVES = 2
TH = T // HALVES
HH = HEADS // HALVES
EXPERTS, GROUPS, TOPK, TOPG = 16, 4, 4, 2
PER_GROUP = EXPERTS // GROUPS
INTER = 176
SHARED = 2 * INTER
ROUTED = EXPERTS * INTER
Q = P // EXPERTS
RTILES = INTER // Q
SH_SIZES = [P, P, SHARED - 2 * P]
SHT = len(SH_SIZES)
UNITS = SHT + RTILES
LAMBDA_INIT = 0.8 - 0.6 * math.exp(-0.3 * 12)
EPS = 1e-5
BIG = 3.0e38

Q_PART = [0, 0, 1, 1, 0, 2]
K_PART = [0, 1, 0, 1, 2, 0]
STACK = len(Q_PART) * D
STACK_DMAS = 16 * 2 * len(Q_PART)

ORDER = [7, 0, 6, 1, 5, 2, 4, 3]
STEPS = HH * NT
GROUP_OF = [1 + (ORDER[s % NT] >= 4) for s in range(STEPS)]
FIRST_GROUP = [sum(GROUP_OF[:s]) for s in range(STEPS)]
GPH = sum(GROUP_OF)

GROUP = [(s, grp) for s in range(STEPS) for grp in range(GROUP_OF[s])]

PHASE = 4
PIECES = 6
UNIT_SHARE = [0.82, 0.895, 1.05, 0.91, 1.046, 0.735, 1.639, 0.906]
PIECE_SHARE = [2.5, 1.0, 1, 1, 1, 1]
LEAD = 8
TILE_AT = {"up_w1": 0, "up_w3": 1, "tanh": 0.5, "silu": 2, "weigh": -1, "hidden": 5,
           "hidden_hi": 6, "hidden_lo": 3, "w2_hi": 2, "w2_lo": 2, "w13_hi": -7.5, "w13_lo": -8.5,
           "down": 8}
STEP_AT = {("scores", False): (0, -25.5), ("scores", True): (-1.5, 1.5),
           ("maxima", False): (1.003, -4.498), ("maxima", True): (-0.997, 2.502),
           ("exponentials", False): (1.502, -0.998), ("exponentials", True): (-0.498, 2.502),
           ("combine", False): 3.5, ("combine", True): 4.5,
           ("transpose", False): (5.9999,), ("transpose", True): (5.4999, 6.9999),
           ("trans_hi", False): (6.5,), ("trans_hi", True): (6, 7.5),
           ("trans_lo", False): (8.5,), ("trans_lo", True): (7, 8.0001),
           ("values", False): (9.0001,), ("values", True): (9.5001, 10.0001),
           ("copy_out", False): 11.4, ("copy_out", True): 11.9}


def by_engine():
    tile = sum(PIECE_SHARE)
    lead = sum(PIECE_SHARE[:LEAD % PIECES]) + LEAD // PIECES * tile
    total = (UNITS + 1) * tile
    shares = [UNIT_SHARE[u % len(UNIT_SHARE)] for u in range(PHASE * (STEPS + 2))]
    marks = [0.0] + [lead + sum(shares[:u]) / sum(shares) * (total - lead) for u in range(len(shares) + 1)] + [total + 100.0]
    units = [-4.0] + list(range(len(shares) + 1)) + [len(shares) + 100.0]

    def at(piece):
        k, r = divmod(piece, PIECES)
        share = k * tile + sum(PIECE_SHARE[:int(r)]) + (r - int(r)) * PIECE_SHARE[int(r)]
        return float(np.interp(share, marks, units))

    order = {"pe": [], "act": [], "dve": [], "pool": []}
    latest = {}

    def place(engine, part, n, where):
        where = max(where, latest.get(part, where))
        latest[part] = where
        order[engine].append((where, part, n))

    for k in range(UNITS):
        for engine, part in (("pe", "up_w1"), ("pe", "up_w3"), ("act", "tanh"), ("dve", "silu"), ("pool", "weigh"), ("dve", "hidden"),
                             ("act", "hidden_hi"), ("pool", "hidden_lo"), ("act", "w2_hi"), ("pool", "w2_lo"), ("act", "w13_hi"),
                             ("pool", "w13_lo")):
            if part != "weigh" or k >= SHT:
                place(engine, part, k, at(PIECES * k + TILE_AT[part]))
        for i in range(TH // P):
            place("pe", "down", k * (TH // P) + i, at(PIECES * k + TILE_AT["down"] + i))
    for s in range(STEPS):
        large = ORDER[s % NT] >= 4
        for engine, part in (("pe", "scores"), ("dve", "maxima"), ("act", "exponentials")):
            for c in range(2):
                place(engine, part, 2 * s + c, PHASE * s + STEP_AT[part, large][c])
        place("dve", "combine", s, PHASE * s + STEP_AT["combine", large])
        for grp in range(GROUP_OF[s]):
            for engine, part in (("pe", "transpose"), ("act", "trans_hi"), ("dve", "trans_lo"), ("pe", "values")):
                place(engine, part, FIRST_GROUP[s] + grp, PHASE * s + STEP_AT[part, large][grp])
        place("act", "copy_out", s, PHASE * s + STEP_AT["copy_out", large])
    return {engine: [(part, n) for _, part, n in sorted(parts, key=lambda p: p[0])] for engine, parts in order.items()}


def size_of(k):
    return SH_SIZES[k] if k < SHT else P


B_ACC, B_UP, B_GATE, B_SCORE, B_TRANS, B_OUT = 0, 2, 3, 4, 6, 7
CREDIT = 2


def build(nc, x, wq, wk, wv, wo, lq1, lk1, lq2, lk2, g, gate_w, bias, w1, w2, w3, sw1, sw2, sw3, out):
    ctx = ExitStack()
    with ctx:
        def sb(name, shape, dt=F32):
            return ctx.enter_context(nc.sbuf_tensor(name, shape, dt))

        def sem(name):
            return ctx.enter_context(nc.semaphore(name))

        qk_parts = nc.dram_tensor("qk_parts", [2, 3, E, T], BF16, kind="Internal").ap()

        xn_hi = sb("xn_hi", [P, KH, T], F32R)
        xn_lo = sb("xn_lo", [P, KH, T], F32R)
        w13 = sb("w13", [P, 2 * KH, ROUTED + SHARED])
        w2r = sb("w2r", [P, UNITS, E])
        wraw = sb("wraw", [P, 4, KH, E])
        w_ring = sb("w_ring", [P, 2, 2, 2 * KH, P], F32R)
        w2_ring = sb("w2_ring", [P, 2, 2, E], F32R)
        v_all = sb("v_all", [P, NT, E])
        v_hi = sb("v_hi", [P, NT, P], F32R)
        v_lo = sb("v_lo", [P, NT, P], F32R)
        cwb = sb("cwb", [P, T])
        cw_half = sb("cw_half", [P, TH])
        qs = sb("qs", [P, 2, 2, T], BF16)
        ks = sb("ks", [P, 2, 2, T], BF16)
        probs = sb("probs", [P, 2, 2, T])
        at_hi = sb("at_hi", [P, 2, BANK], F32R)
        at_lo = sb("at_lo", [P, 2, BANK], F32R)
        hid = sb("hid", [P, 2, TH])
        h_hi = sb("h_hi", [P, 2, TH], F32R)
        h_lo = sb("h_lo", [P, 2, TH], F32R)
        ot = sb("ot", [P, HALVES, T])
        gate = sb("gate", [P, NT, E])
        ident = sb("ident", [P, P])
        ident_bf = sb("ident_bf", [P, P], BF16)
        causal = sb("causal", [P, P], BF16)
        lower16 = sb("lower16", [P, EXPERTS, EXPERTS])
        negmax = sb("negmax", [P, 4, 2])
        coef = sb("coef", [P, 4, 2])
        sums = sb("sums", [P, 2, HALVES, STEPS])
        gcol = sb("gcol", [P, 2])
        gw_raw = sb("gw_raw", [EXPERTS, E])
        gwt = sb("gwt", [P, 2, KH, EXPERTS], F32R)
        bias_b = sb("bias_b", [P, EXPERTS])
        lams = sb("lams", [P, 4, D])
        lam_t = sb("lam_t", [P, 8])
        stats = sb("stats", [P, NT, 6])
        mv = sb("mv", [P, NT, 2])
        ln_t = sb("ln_t", [P, 4, NT])

        ps = ctx.enter_context(nc.psum_tensor("ps", [P, 8 * BANK], F32))

        def bank(b, n=1, rows=P):
            return ps[0:rows, b * BANK:(b + n) * BANK]

        small = wraw[:, 0:2].rearrange("p n k e -> p (n k e)").rearrange("p (n t) -> p n t", n=8)
        xt = probs[:, 0].rearrange("p c (i e) -> p (c i) e", e=E)
        rank_a = probs[:, 0, 0].bitcast(BF16)
        rank_b = probs[:, 0, 1].bitcast(BF16)
        cw_rep = probs[:, 0, 0].rearrange("p (i r) -> p i r", r=P)
        resid = [cwb[:, 0:BANK], cwb[:, BANK:], cw_half[:, :], hid[:, 1]]
        lg_t = hid[:, 0]
        stage = [t[:, 0:3 * T].rearrange("p (a t) -> p a t", a=3) for t in
                 (ot[:, :, :].rearrange("p a b -> p (a b)").bitcast(BF16), gate[:, :, :].rearrange("p a b -> p (a b)").bitcast(BF16),
                  probs[:, 1].rearrange("p a b -> p (a b)").bitcast(BF16), qs[:, :, :, :].rearrange("p a c t -> p (a c t)"))]
        sel_g = small[:, 0, 0:NT * GROUPS].rearrange("p (i a) -> p i a", a=GROUPS)

        def table(n):
            return small[:, n].rearrange("p (i e) -> p i e", e=EXPERTS)

        s_x1, s_wqkv, s_gatew, s_vecs, s_sh, s_w13, s_w2, s_wo = map(
            sem, ["x_in", "wqkv_in", "gate_in", "vecs_in", "shared_in", "w13_in", "w2_in", "wo_in"])
        s_x = [s_x1, sem("x_in_2")]
        s_const = sem("const_made")
        s_link_v, s_link_p, s_link_a = sem("vector_link"), sem("pool_link"), sem("scalar_link")
        s_var, s_std, s_xn, s_xt, s_xhi, s_xlo = map(
            sem, ["var_ready", "std_ready", "xn_ready", "xn_transposed", "xn_hi_ready", "xn_lo_ready"])
        s_gwt_ps, s_gwt_hi, s_gwt = sem("gate_transposed"), sem("gate_hi_ready"), sem("gate_parts_ready")
        s_phi, s_plo = sem("proj_hi_ready"), sem("proj_lo_ready")
        s_proj, s_part0, s_resid, s_part1, s_parts = map(sem, ["proj_done", "part0_ready", "resid_ready", "part1_ready", "parts_ready"])
        s_stored = [sem(f"parts_stored_{n}") for n in range(4)]
        s_v = sem("v_ready")
        s_lgt, s_lgc, s_lg, s_el, s_cwrep, s_cwt, s_cwb = map(
            sem, ["logits_t_done", "logits_t_copied", "logits_done", "exp_logits_ready", "weights_ready",
                  "weights_transposed", "weights_spread"])
        s_dot, s_edot, s_lam = sem("lambda_dots"), sem("lambda_exps"), sem("lambda_ready")

        s_w13hi, s_w13lo, s_w2hi, s_w2lo = map(sem, ["w13_hi_split", "w13_lo_split", "w2_hi_split", "w2_lo_split"])
        s_a, s_b, s_th, s_u, s_uc, s_h, s_hhi, s_hlo, s_down = map(
            sem, ["w1_product", "w3_product", "tanh_ready", "silu_ready", "weighted_ready", "hidden_ready",
                  "hidden_hi", "hidden_lo", "down_done"])
        s_accth, s_accfree = sem("acc_tanh"), sem("acc_free")
        s_stack = [sem(f"stacks_in_{n}") for n in range(2)]
        s_score, s_negmax, s_prob, s_chain, s_comb = map(
            sem, ["scores_done", "negmax_ready", "probs_ready", "coef_chain", "combined"])
        s_trans, s_athi, s_atlo, s_pv, s_oev = map(
            sem, ["transposed", "trans_hi", "trans_lo", "pv_done", "out_copied"])
        s_vhi, s_vlo = sem("v_hi_split"), sem("v_lo_split")
        s_cwhalf = sem("weights_of_half")
        s_xre, s_sq, s_ss, s_fac, s_sdf, s_frep, s_fps, s_on, s_onhi, s_onlo, s_wohi, s_wolo, s_so, s_res, s_out = map(
            sem, ["x_again", "squares", "sum_squares", "var_of_heads", "std_of_heads", "factors", "factors_t",
                  "normed", "normed_hi", "normed_lo", "wo_hi", "wo_lo", "attn_out", "result", "stored"])

        tail = w13[:, :, :].rearrange("p a b -> p (a b)")
        x_again = tail[:, 0:NT * E].rearrange("p (i e) -> p i e", e=E)
        squares = tail[:, 2048:4096].rearrange("p (a t) -> p a t", a=HALVES)
        frep = tail[:, 4096:6144].rearrange("p (a i h r) -> p a i h r", a=HALVES, h=HH, r=DV)
        normed = tail[:, 6144:8192].rearrange("p (a t) -> p a t", a=HALVES)
        result = tail[:, 8192:10240].rearrange("p (i e) -> p i e", e=E)
        fac = tail[:, 10240:10240 + 4 * NT * HEADS].rearrange("p (n a h i) -> p n a h i", n=4, a=HALVES, i=NT)
        head_ones = tail[:, 10496:10500]

        def three(pe_out, a_hi, a_lo, b_hi, b_lo, first, last, skip=False):
            nc.tensor.matmul(pe_out, a_hi, b_hi, start=first, stop=False, skip_group_check=skip)
            nc.tensor.matmul(pe_out, a_hi, b_lo, start=False, stop=False, skip_group_check=skip)
            return nc.tensor.matmul(pe_out, a_lo, b_hi, start=False, stop=last, skip_group_check=skip)

        def proj_w(slot, part, kh):
            return w_ring[:, slot, part].rearrange("p m n -> p (m n)")[:, kh * E:(kh + 1) * E]

        def raw_tile(k):
            if k < SHT:
                return w13[:, :, ROUTED + k * P:ROUTED + k * P + size_of(k)]
            return w13[:, :, 0:ROUTED].rearrange("p m (e h) -> p m e h", h=INTER)[:, :, :, (k - SHT) * Q:(k - SHT + 1) * Q]

        def ring_tile(k, part, dt=None):
            t = w_ring[:, k % 2, part, :, 0:size_of(k)]
            t = t if dt is None else t.bitcast(dt)
            return t if k < SHT else t.rearrange("p m (e q) -> p m e q", q=Q)

        order = by_engine()

        block = ctx.enter_context(nc.Block())

        @block.sync
        def _(sp):
            xv = x.rearrange("o (i p) e -> p (o i) e", p=P)
            for half in range(2):
                sp.dma_start(xt[:, half * 4:half * 4 + 4], xv[:, half * 4:half * 4 + 4]).then_inc(s_x[half], 16)
            sp.dma_start(gw_raw[:, :], gate_w).then_inc(s_gatew, 16)
            for n, w in enumerate((wq, wk, wv)):
                sp.dma_start(wraw[:, n], w.rearrange("(k p) e -> p k e", p=P)).then_inc(s_wqkv, 16)
            for n, v in enumerate((lq1, lk1, lq2, lk2)):
                sp.dma_start(lams[:, n], v.rearrange("(o d) -> o d", o=1).to_broadcast([P, D])).then_inc(s_vecs, 16)
            sp.dma_start(bias_b[:, :], bias.rearrange("(o d) -> o d", o=1).to_broadcast([P, EXPERTS])).then_inc(s_vecs, 16)
            for n in range(HH):
                sp.dma_start(gcol[n * DV:(n + 1) * DV, 0:1], g.rearrange("(d o) -> d o", o=1)).then_inc(s_vecs, 16)
            for m, w in enumerate((sw1, sw3)):
                sp.dma_start(w13[:, m * KH:(m + 1) * KH, ROUTED:], w.rearrange("(k p) h -> p k h", p=P)).then_inc(s_sh, 16)
            sp.dma_start(w2r[:, 0:2, :], sw2[0:2 * P].rearrange("(s p) e -> p s e", p=P)).then_inc(s_sh, 16)
            sp.dma_start(w2r[0:SH_SIZES[2], 2, :], sw2[2 * P:]).then_inc(s_sh, 16)
            for m, w in enumerate((w1, w3)):
                for kh in range(KH):
                    sp.dma_start(w13[:, m * KH + kh, 0:ROUTED].rearrange("p (e h) -> p e h", h=INTER),
                                 w[:, kh * P:(kh + 1) * P, :].rearrange("e p h -> p e h")).then_inc(s_w13, 16)
            for e in range(EXPERTS):
                sp.dma_start(w2r[e * Q:(e + 1) * Q, SHT:, :], w2[e].rearrange("(j q) d -> q j d", q=Q)).then_inc(s_w2, 16)
            sp.dma_start(wraw[:, 3], wo.rearrange("(k p) e -> p k e", p=P)).then_inc(s_wo, 16)
            for n in range(4):
                sp.wait_ge(s_parts, 2 * n + 2)
                sp.dma_start(qk_parts[n // 2, :, (n % 2) * P:(n % 2 + 1) * P, :].rearrange("a p t -> p a t"),
                             stage[n]).then_inc(s_stored[n], 16)
            for n in range(4):
                sp.wait_ge(s_stored[n], 16)
            rows = qk_parts.rearrange("s a (f h c d) t -> (s a f h) d c t", f=HALVES, h=HH, c=2)
            with sp.Fori(0, HALVES) as hf:
                for a in range(HH):
                    sp.wait_ge(s_score, hf * (2 * STEPS) + (2 * NT * (a - 1) + CREDIT + 2 * NT))
                    for n in range(2):
                        stack = (qs, ks)[n]
                        for r, part in enumerate((Q_PART, K_PART)[n]):
                            row = ((n * 3 + part) * HALVES) * HH + a
                            sp.dma_start(stack[r * D:(r + 1) * D, a % 2],
                                         rows[bass.ds(hf * HH + row, 1)].rearrange("o d c t -> (o d) c t")).then_inc(s_stack[a % 2], 16)
            sp.wait_ge(s_fac, 1)
            sp.dma_start(x_again, xv).then_inc(s_xre, 16)
            for i in range(NT):
                sp.wait_ge(s_res, i + 1)
                sp.dma_start(out.rearrange("o (i p) e -> p (o i) e", p=P)[:, i], result[:, i]).then_inc(s_out, 16)
            sp.wait_ge(s_out, 16 * NT)

        @block.tensor
        def _(pe):
            pe.sem_inc(s_a, CREDIT)
            pe.sem_inc(s_b, CREDIT)
            pe.sem_inc(s_down, CREDIT)
            pe.sem_inc(s_trans, 1)
            pe.sem_inc(s_pv, CREDIT)
            pe.sem_inc(s_score, CREDIT + 2 * NT)
            pe.wait_ge(s_const, 1)
            pe.wait_ge(s_gatew, 16)
            for kh in range(KH):
                last = nc.tensor.transpose(ps[:, 3 * BANK + kh * EXPERTS:3 * BANK + (kh + 1) * EXPERTS],
                                           gw_raw[:, kh * P:(kh + 1) * P], ident[0:EXPERTS, 0:EXPERTS])
            last.then_inc(s_gwt_ps, 1)
            for i in range(NT):
                pe.wait_ge(s_xn, i + 1)
                for kh in range(KH):
                    b = 4 + 2 * (i // 4) + kh
                    last = nc.tensor.transpose(ps[:, b * BANK + (i % 4) * P:b * BANK + (i % 4 + 1) * P],
                                               xt[:, i, kh * P:(kh + 1) * P], ident[:, :])
                last.then_inc(s_xt, 1)
            pe.wait_ge(s_gwt, 1)
            pe.wait_ge(s_xhi, 4)
            pe.wait_ge(s_xlo, 4)
            for c in range(2):
                for kh in range(KH):
                    last = three(bank(4 + c, rows=EXPERTS), gwt[:, 0, kh], gwt[:, 1, kh],
                                 xn_hi[:, kh, c * TH:(c + 1) * TH], xn_lo[:, kh, c * TH:(c + 1) * TH], kh == 0, kh == KH - 1)
                last.then_inc(s_lgt, 1)
            for r in range(8):
                n, mt, c = r // 4, (r // 2) % 2, r % 2
                if r % 4 == 0:
                    pe.wait_ge(s_phi, n + 1)
                    pe.wait_ge(s_plo, n + 1)
                if r >= 4:
                    pe.wait_ge(s_resid, r - 3)
                for kh in range(KH):
                    last = three(bank(r % 4), proj_w(n, 0, kh)[:, mt * P:(mt + 1) * P], proj_w(n, 1, kh)[:, mt * P:(mt + 1) * P],
                                 xn_hi[:, kh, c * TH:(c + 1) * TH], xn_lo[:, kh, c * TH:(c + 1) * TH], kh == 0, kh == KH - 1)
                last.then_inc(s_proj, 1)
                if r == 0:
                    for i in range(NT):
                        if i % 4 == 0:
                            pe.wait_ge(s_lgc, i // 4 + 1)
                        at = (6 + i // 4) * BANK + (i % 4) * EXPERTS
                        last = nc.tensor.transpose(ps[:, at:at + EXPERTS],
                                                   lg_t[32 * (i // 4):32 * (i // 4) + EXPERTS, (i % 4) * P:(i % 4 + 1) * P],
                                                   ident[32 * (i // 4):32 * (i // 4) + EXPERTS, 32 * (i // 4):32 * (i // 4) + EXPERTS])
                    last.then_inc(s_lg, 1)
            for r in range(8, 12):
                if r == 8:
                    pe.wait_ge(s_phi, 3)
                    pe.wait_ge(s_plo, 3)
                pe.wait_ge(s_resid, r - 3)
                for i in (2 * (r - 8), 2 * (r - 8) + 1):
                    for kh in range(KH):
                        last = three(ps[:, (r % 4) * BANK + (i % 2) * E:(r % 4) * BANK + (i % 2 + 1) * E],
                                     xn_hi[:, kh, i * P:(i + 1) * P], xn_lo[:, kh, i * P:(i + 1) * P],
                                     proj_w(0, 0, kh), proj_w(0, 1, kh), kh == 0, kh == KH - 1)
                last.then_inc(s_proj, 1)
            pe.wait_ge(s_cwrep, 1)
            for i in range(NT):
                last = nc.tensor.transpose(ps[:, 4 * BANK + i * P:4 * BANK + (i + 1) * P], cw_rep[:, i], ident[:, :])
            last.then_inc(s_cwt, 1)
            pe.wait_ge(s_v, 4)
            pe.wait_ge(s_cwb, 1)
            pe.wait_ge(s_el, 1)

            with pe.Fori(0, HALVES) as hf:
                u0 = hf * UNITS
                n0 = hf * STEPS

                def up(k, m13):
                    m = size_of(k)
                    if m13 == 0:
                        pe.wait_ge(s_w13hi, u0 + (k + 1 + CREDIT))
                        pe.wait_ge(s_w13lo, u0 + (k + 1 + CREDIT))
                        pe.wait_ge(s_u, u0 + (k + CREDIT))
                    else:
                        pe.wait_ge(s_h, u0 + (k + CREDIT))
                    for kh in range(KH):
                        last = three(bank(B_UP + m13, rows=m), w_ring[:, k % 2, 0, m13 * KH + kh, 0:m],
                                     w_ring[:, k % 2, 1, m13 * KH + kh, 0:m], xn_hi[:, kh, bass.ds(hf * TH, TH)],
                                     xn_lo[:, kh, bass.ds(hf * TH, TH)], kh == 0, kh == KH - 1)
                    last.then_inc((s_a, s_b)[m13], 1)

                def down(k, i):
                    m = size_of(k)
                    if i == 0:
                        pe.wait_ge(s_hhi, u0 + (k + 1 + CREDIT))
                        pe.wait_ge(s_hlo, u0 + (k + 1 + CREDIT))
                        pe.wait_ge(s_w2hi, u0 + (k + 1 + CREDIT))
                        pe.wait_ge(s_w2lo, u0 + (k + 1 + CREDIT))
                        if k == 0:
                            pe.wait_ge(s_accfree, hf + 1)
                    at = B_ACC * BANK + i * E
                    last = three(ps[:, at:at + E], h_hi[0:m, k % 2, i * P:(i + 1) * P], h_lo[0:m, k % 2, i * P:(i + 1) * P],
                                 w2_ring[0:m, k % 2, 0], w2_ring[0:m, k % 2, 1], k == 0 and i % 2 == 0, k == UNITS - 1, skip=True)
                    if i == TH // P - 1:
                        last.then_inc(s_down, 1)

                def scores(s, c):
                    a, i = s // NT, ORDER[s % NT]
                    if c == 0 and s % NT == 0:
                        pe.wait_ge(s_stack[a % 2], hf * (HH // 2 * STACK_DMAS) + STACK_DMAS * (a // 2 + 1))
                    behind = 1 if (i < 4 and c == 1) else 0
                    pe.wait_ge(s_prob, n0 * 2 + (2 * s + c - behind + CREDIT))
                    w = (i + 1) * P
                    q = qs[0:STACK, a % 2, c, i * P:(i + 1) * P]
                    at = (B_SCORE + (c if i < 4 else 0)) * BANK
                    for lo in range(0, w, BANK):
                        hi = min(lo + BANK, w)
                        diagonal = hi == w
                        nc.tensor.matmul(ps[:, at + lo:at + hi], q, ks[0:STACK, a % 2, c, lo:hi], start=True, stop=not diagonal)
                        if diagonal:
                            last = nc.tensor.matmul(ps[:, at + w - P:at + w], ident_bf[:, :], causal[:, :], start=False, stop=True)
                    last.then_inc(s_score, 1)

                def transposes(s, grp):
                    i = ORDER[s % NT]
                    gi = FIRST_GROUP[s] + grp
                    if grp == 0:
                        pe.wait_ge(s_comb, n0 + (s + 1 + CREDIT))
                    pe.wait_ge(s_atlo, hf * GPH + (gi + CREDIT))
                    for j in range(4 * grp, min(4 * grp + 4, i + 1)):
                        last = nc.tensor.transpose(ps[:, B_TRANS * BANK + (j % 4) * P:B_TRANS * BANK + (j % 4 + 1) * P],
                                                   probs[:, s % 2, 0, j * P:(j + 1) * P], ident[:, :])
                    last.then_inc(s_trans, 1)

                def values(s, grp):
                    a, i = s // NT, ORDER[s % NT]
                    gi = FIRST_GROUP[s] + grp
                    if s == 0 and grp == 0:
                        pe.wait_ge(s_vhi, hf + 1)
                        pe.wait_ge(s_vlo, hf + 1)
                    if grp == 0:
                        pe.wait_ge(s_oev, n0 + (s + CREDIT))
                    pe.wait_ge(s_athi, hf * GPH + (gi + 1 + CREDIT))
                    pe.wait_ge(s_atlo, hf * GPH + (gi + 1 + CREDIT))
                    for j in range(4 * grp, min(4 * grp + 4, i + 1)):
                        last = three(ps[0:DV, B_OUT * BANK:B_OUT * BANK + P], v_hi[:, j, a * DV:(a + 1) * DV], v_lo[:, j, a * DV:(a + 1) * DV],
                                     at_hi[:, gi % 2, (j % 4) * P:(j % 4 + 1) * P], at_lo[:, gi % 2, (j % 4) * P:(j % 4 + 1) * P],
                                     j == 0, j == i)
                    last.then_inc(s_pv, 1)

                for part, n in order["pe"]:
                    if part == "up_w1":
                        up(n, 0)
                    elif part == "up_w3":
                        up(n, 1)
                    elif part == "down":
                        down(*divmod(n, TH // P))
                    elif part == "scores":
                        scores(*divmod(n, 2))
                    elif part == "transpose":
                        transposes(*GROUP[n])
                    elif part == "values":
                        values(*GROUP[n])

            for hf in range(HALVES):
                pe.wait_ge(s_sq, hf + 1)
                for i in range(NT):
                    at = (4 + hf) * BANK + i * HH
                    last = nc.tensor.matmul(ps[:, at:at + HH], squares[:, hf, i * P:(i + 1) * P], head_ones, start=True, stop=True)
                last.then_inc(s_ss, 1)
            pe.wait_ge(s_accfree, 3)
            for hf in range(HALVES):
                pe.wait_ge(s_frep, hf + 1)
                for i in range(NT):
                    at = 2 * hf * BANK + i * P
                    last = nc.tensor.transpose(ps[:, at:at + P], frep[:, hf, i].rearrange("p h r -> p (h r)"), ident[:, :])
                last.then_inc(s_fps, 1)
            pe.wait_ge(s_wohi, 1)
            pe.wait_ge(s_wolo, 1)
            pe.wait_ge(s_fac, 1 + HALVES)
            for kh in range(KH):
                pe.wait_ge(s_onhi, kh + 1)
                pe.wait_ge(s_onlo, kh + 1)
                for i in range(NT):
                    b = 4 + i // 2
                    last = three(ps[:, b * BANK + (i % 2) * E:b * BANK + (i % 2 + 1) * E],
                                 xn_hi[:, kh, i * P:(i + 1) * P], xn_lo[:, kh, i * P:(i + 1) * P],
                                 proj_w(1, 0, kh), proj_w(1, 1, kh), kh == 0 and i % 2 == 0, kh == KH - 1, skip=True)
                    if kh == KH - 1 and i % 2 == 1:
                        last.then_inc(s_so, 1)

        @block.scalar
        def _(act):
            for s in (s_w13hi, s_w2hi, s_th, s_hhi, s_prob, s_athi, s_oev):
                act.sem_inc(s, CREDIT)

            def split_hi(n):
                slot = (0, 1, 0, 1)[n]
                return nc.scalar.activation(w_ring[:, slot, 0].rearrange("p m n -> p (m n)"),
                                            wraw[:, n].rearrange("p k e -> p (k e)"), ACT.Copy)

            act.wait_ge(s_gwt_ps, 1)
            nc.scalar.activation(gwt[:, 0].rearrange("p k e -> p (k e)"), ps[:, 3 * BANK:3 * BANK + KH * EXPERTS], ACT.Copy).then_inc(s_gwt_hi, 1)
            act.wait_ge(s_wqkv, 48)
            split_hi(0).then_inc(s_phi, 1)
            split_hi(1).then_inc(s_phi, 1)
            act.wait_ge(s_var, 1)
            nc.scalar.activation(ln_t[:, 1], ln_t[:, 0], ACT.Sqrt).then_inc(s_std, 1)
            act.wait_ge(s_dot, 1)
            nc.scalar.activation(lam_t[:, 2:4], lam_t[:, 0:2], ACT.Exp).then_inc(s_edot, 1)
            for c in range(2):
                act.wait_ge(s_xt, 4 * c + 4)
                for kh in range(KH):
                    nc.scalar.activation(xn_hi[:, kh, c * TH:(c + 1) * TH], bank(4 + 2 * c + kh), ACT.Copy).then_inc(s_xhi, 1)
            for c in range(2):
                act.wait_ge(s_lgt, c + 1)
                nc.scalar.activation(lg_t[32 * c:32 * c + EXPERTS, :], bank(4 + c, rows=EXPERTS), ACT.Copy).then_inc(s_lgc, 1)

            def part_0(r):
                act.wait_ge(s_proj, r + 1)
                nc.scalar.activation(stage[r // 2][:, 0, r % 2 * TH:(r % 2 + 1) * TH], bank(r % 4), ACT.Copy,
                                     scale=D ** -0.5 if r < 4 else 1.0).then_inc(s_part0, 1)

            def part_1(r):
                act.wait_ge(s_resid, r + 1)
                nc.scalar.activation(stage[r // 2][:, 1, r % 2 * TH:(r % 2 + 1) * TH], resid[r % 4], ACT.Copy).then_inc(s_part1, 1)

            part_0(0)
            act.wait_ge(s_plo, 2)
            act.wait_ge(s_lg, 1)
            nc.scalar.activation(small[:, 1].rearrange("p (b n) -> p b n", b=2), bank(6, 2).rearrange("p (b n) -> p b n", b=2)[:, :, 0:4 * EXPERTS],
                                 ACT.Exp, scale=-1.0).then_inc(s_el, 1)
            for r in range(1, 9):
                if r < 8:
                    part_0(r)
                part_1(r - 1)
                if r == 4:
                    split_hi(2).then_inc(s_phi, 1)
            for r in range(4):
                act.wait_ge(s_proj, 9 + r)
                nc.scalar.activation(v_all[:, 2 * r:2 * r + 2].rearrange("p i e -> p (i e)"), bank(r % 4), ACT.Copy).then_inc(s_v, 1)
            act.wait_ge(s_parts, 8)
            act.wait_ge(s_cwt, 1)
            nc.scalar.activation(cwb[:, :], bank(4, 2), ACT.Copy).then_inc(s_cwb, 1)
            act.wait_ge(s_v, 4)
            act.wait_ge(s_cwb, 1)

            with act.Fori(0, HALVES) as hf:
                u0 = hf * UNITS
                n0 = hf * STEPS

                def split_w13(k):
                    if k == SHT:
                        act.wait_ge(s_w13, 64)
                    act.wait_ge(s_b, u0 + (k + 1))
                    nc.scalar.activation(ring_tile(k, 0), raw_tile(k), ACT.Copy).then_inc(s_w13hi, 1)

                def split_w2(k):
                    m = size_of(k)
                    if k == SHT:
                        act.wait_ge(s_w2, 256)
                    act.wait_ge(s_down, u0 + (k + 1))
                    nc.scalar.activation(w2_ring[0:m, k % 2, 0], w2r[0:m, k], ACT.Copy).then_inc(s_w2hi, 1)

                def high_hidden(k):
                    m = size_of(k)
                    act.wait_ge(s_h, u0 + (k + 1 + CREDIT))
                    act.wait_ge(s_down, u0 + (k + 1))
                    nc.scalar.activation(h_hi[0:m, k % 2], hid[0:m, k % 2], ACT.Copy).then_inc(s_hhi, 1)

                def tanh(k):
                    m = size_of(k)
                    act.wait_ge(s_a, u0 + (k + 1 + CREDIT))
                    act.wait_ge(s_hlo, u0 + (k - 1 + CREDIT))
                    nc.scalar.activation(hid[0:m, k % 2], bank(B_UP, rows=m), ACT.Tanh, scale=0.5).then_inc(s_th, 1)

                def exponentials(s, c):
                    i = ORDER[s % NT]
                    w = (i + 1) * P
                    at = (B_SCORE + (c if i < 4 else 0)) * BANK
                    act.wait_ge(s_negmax, n0 * 2 + (2 * s + c + 1))
                    if c == 0:
                        act.wait_ge(s_trans, hf * GPH + (FIRST_GROUP[s - 1] + 1 if s else 1 - 0))
                    nc.scalar.activation(probs[:, s % 2, c, 0:w], ps[:, at:at + w], ACT.Exp, bias=negmax[:, s % 4, c:c + 1],
                                         accum_out=sums[:, c, bass.ds(hf, 1), s]).then_inc(s_prob, 1)

                def copy_trans(s, grp):
                    gi = FIRST_GROUP[s] + grp
                    w = min(BANK, (ORDER[s % NT] + 1 - 4 * grp) * P)
                    act.wait_ge(s_trans, hf * GPH + (gi + 2))
                    act.wait_ge(s_pv, hf * GPH + (gi + 1))
                    nc.scalar.activation(at_hi[:, gi % 2, 0:w], ps[:, B_TRANS * BANK:B_TRANS * BANK + w], ACT.Copy).then_inc(s_athi, 1)

                def copy_out(s):
                    a, i = s // NT, ORDER[s % NT]
                    act.wait_ge(s_pv, hf * GPH + (FIRST_GROUP[s] + GROUP_OF[s] + CREDIT))
                    nc.scalar.activation(ot[a * DV:(a + 1) * DV, bass.ds(hf, 1), i * P:(i + 1) * P].rearrange("p o t -> p (o t)"),
                                         ps[0:DV, B_OUT * BANK:B_OUT * BANK + P], ACT.Copy).then_inc(s_oev, 1)

                act.wait_ge(s_pv, hf * GPH + CREDIT)
                nc.scalar.activation(v_hi[:, :, :], v_all[:, :, bass.ds(hf * P, P)], ACT.Copy).then_inc(s_vhi, 1)
                act.wait_ge(s_uc, hf * RTILES + 1)
                nc.scalar.activation(cw_half[:, :], cwb[:, bass.ds(hf * TH, TH)], ACT.Copy).then_inc(s_cwhalf, 1)
                act.wait_ge(s_sh, 64)
                for part, n in order["act"]:
                    if part == "w13_hi":
                        split_w13(n)
                    elif part == "w2_hi":
                        split_w2(n)
                    elif part == "tanh":
                        tanh(n)
                    elif part == "hidden_hi":
                        high_hidden(n)
                    elif part == "exponentials":
                        exponentials(*divmod(n, 2))
                    elif part == "trans_hi":
                        copy_trans(*GROUP[n])
                    elif part == "copy_out":
                        copy_out(n)
                act.wait_ge(s_down, u0 + (UNITS + CREDIT))
                act.wait_ge(s_trans, hf * GPH + (GPH + 1))
                nc.scalar.activation(probs[:, 0, 0], bank(B_ACC, 2), ACT.Tanh, scale=0.5).then_inc(s_accth, 1)

            act.wait_ge(s_oev, HALVES * STEPS + CREDIT)
            act.wait_ge(s_fac, 1)
            for hf in range(HALVES):
                nc.scalar.activation(squares[:, hf], ot[:, hf], ACT.Square).then_inc(s_sq, 1)
            act.wait_ge(s_wo, 16)
            act.wait_ge(s_b, HALVES * UNITS + CREDIT)
            split_hi(3).then_inc(s_wohi, 1)
            for hf in range(HALVES):
                act.wait_ge(s_fac, 2 + hf)
                nc.scalar.activation(fac[:, 2, hf], fac[:, 1, hf], ACT.Sqrt).then_inc(s_sdf, 1)
            for hf in range(HALVES):
                act.wait_ge(s_on, hf + 1)
                nc.scalar.activation(xn_hi[:, hf], normed[:, hf], ACT.Copy).then_inc(s_onhi, 1)

        @block.vector
        def _(dve):
            links = [0]

            def link(ins):
                links[0] += 1
                ins.then_inc(s_link_v, 1)
                dve.wait_ge(s_link_v, links[0])

            for s in (s_u, s_h, s_comb, s_atlo):
                dve.sem_inc(s, CREDIT)
            dve.sem_inc(s_accfree, 1)
            for i in range(NT):
                if i % 4 == 0:
                    dve.wait_ge(s_x[i // 4], 16)
                last = nc.vector.bn_stats(stats[:, i], xt[:, i])
            link(last)
            for i in range(NT):
                last = nc.vector.bn_aggr(mv[:, i], stats[:, i])
            link(last)
            nc.vector.tensor_scalar(ln_t[:, 0], mv[:, :, 1], EPS, None, ALU.add).then_inc(s_var, 1)
            dve.wait_ge(s_std, 1)
            link(nc.vector.reciprocal(ln_t[:, 1], ln_t[:, 1]))
            link(nc.vector.tensor_tensor(ln_t[:, 2], ln_t[:, 1], ln_t[:, 1], ALU.mult))
            link(nc.vector.tensor_tensor(ln_t[:, 2], ln_t[:, 2], ln_t[:, 0], ALU.mult))
            link(nc.vector.tensor_scalar(ln_t[:, 2], ln_t[:, 2], -0.5, 1.5, ALU.mult, ALU.add))
            link(nc.vector.tensor_tensor(ln_t[:, 1], ln_t[:, 1], ln_t[:, 2], ALU.mult))
            for i in range(NT):
                nc.vector.tensor_scalar(xt[:, i], xt[:, i], mv[:, i, 0:1], ln_t[:, 1, i:i + 1], ALU.subtract, ALU.mult).then_inc(s_xn, 1)
            dve.wait_ge(s_vecs, 144)
            for n in range(2):
                link(nc.vector.tensor_tensor(lams[:, 2 * n], lams[:, 2 * n], lams[:, 2 * n + 1], ALU.mult))
                last = nc.vector.tensor_reduce(lam_t[:, n:n + 1], lams[:, 2 * n], axis=X, op=ALU.add)
            last.then_inc(s_dot, 1)
            dve.wait_ge(s_edot, 1)
            nc.vector.scalar_tensor_tensor(lam_t[:, 4:5], lam_t[:, 3:4], -LAMBDA_INIT, lam_t[:, 2:3], ALU.add, ALU.subtract).then_inc(s_lam, 1)
            nc.vector.tensor_scalar(gcol[:, 1:2], gcol[:, 0:1], 1.0 - LAMBDA_INIT, None, ALU.mult).then_inc(s_lam, 1)
            dve.wait_ge(s_gwt_hi, 1)
            nc.vector.tensor_tensor(gwt[:, 1].rearrange("p k e -> p (k e)"), ps[:, 3 * BANK:3 * BANK + KH * EXPERTS],
                                    gwt[:, 0].bitcast(F32).rearrange("p k e -> p (k e)"), ALU.subtract).then_inc(s_gwt, 1)
            for r in range(4):
                c, kh = r // 2, r % 2
                dve.wait_ge(s_xhi, r + 1)
                nc.vector.tensor_tensor(xn_lo[:, kh, c * TH:(c + 1) * TH], bank(4 + r),
                                        xn_hi[:, kh, c * TH:(c + 1) * TH].bitcast(F32), ALU.subtract).then_inc(s_xlo, 1)

            def remainder(r):
                dve.wait_ge(s_part0, r + 1)
                if r >= 4:
                    dve.wait_ge(s_parts, r - 3)
                nc.vector.scalar_tensor_tensor(resid[r % 4], bank(r % 4), D ** -0.5 if r < 4 else 1.0,
                                               stage[r // 2][:, 0, r % 2 * TH:(r % 2 + 1) * TH], ALU.mult, ALU.subtract).then_inc(s_resid, 1)

            sig, sc, masked, sel = table(2), table(3), table(4), table(5)
            remainder(0)
            dve.wait_ge(s_el, 1)
            link(nc.vector.tensor_scalar(small[:, 1], small[:, 1], 1.0, None, ALU.add))
            link(nc.vector.reciprocal(small[:, 2], small[:, 1]))
            remainder(1)
            link(nc.vector.tensor_tensor(sc, sig, bias_b[:, :].rearrange("p (o e) -> p o e", o=1).to_broadcast([P, NT, EXPERTS]), ALU.add))
            gmax = small[:, 6, 0:NT * GROUPS].rearrange("p (i a) -> p i a", a=GROUPS)
            link(nc.vector.tensor_reduce(gmax, small[:, 3].rearrange("p (i a e) -> p i a e", a=GROUPS, e=PER_GROUP), axis=X, op=ALU.max))

            dve.wait_ge(s_const, 2)

            def rank(out, values, n, tmp_a, tmp_b, tile0, tiles, between=()):
                shape = [P, tiles, n, n]
                mine = values[:, tile0:tile0 + tiles].rearrange("p i (e o) -> p i e o", o=1).to_broadcast(shape)
                theirs = values[:, tile0:tile0 + tiles].rearrange("p i (o e) -> p i o e", o=1).to_broadcast(shape)
                lower = lower16[:, 0:n, 0:n].rearrange("p (o e) f -> p o e f", o=1).to_broadcast(shape)
                a = tmp_a[:, 0:tiles * n * n].rearrange("p (i e f) -> p i e f", e=n, f=n)
                b = tmp_b[:, 0:tiles * n * n].rearrange("p (i e f) -> p i e f", e=n, f=n)
                nc.vector.tensor_tensor(a, theirs, mine, ALU.is_gt)
                for r in between[0:1]:
                    remainder(r)
                link(nc.vector.tensor_tensor(b, theirs, mine, ALU.is_ge))
                for r in between[1:2]:
                    remainder(r)
                link(nc.vector.tensor_tensor(b, b, lower, ALU.mult))
                for r in between[2:]:
                    remainder(r)
                link(nc.vector.tensor_tensor(a, a, b, ALU.max))
                link(nc.vector.tensor_reduce(out[:, tile0:tile0 + tiles], a, axis=X, op=ALU.add))

            rank(sel_g, gmax, GROUPS, rank_a, rank_b, 0, NT)
            remainder(2)
            remainder(3)
            link(nc.vector.tensor_scalar(small[:, 0, 0:NT * GROUPS], small[:, 0, 0:NT * GROUPS], float(TOPG), None, ALU.is_lt))
            link(nc.vector.tensor_scalar(small[:, 6, 0:NT * GROUPS], small[:, 0, 0:NT * GROUPS], 1.0, BIG, ALU.subtract, ALU.mult))

            def by_expert(t):
                return t.rearrange("p (i a o) -> p (i a) o", a=GROUPS, o=1).to_broadcast([P, NT * GROUPS, PER_GROUP])

            m3 = small[:, 4].rearrange("p (i e) -> p i e", e=PER_GROUP)
            link(nc.vector.tensor_tensor(m3, small[:, 3].rearrange("p (i e) -> p i e", e=PER_GROUP), by_expert(small[:, 0, 0:NT * GROUPS]), ALU.mult))
            link(nc.vector.tensor_tensor(m3, m3, by_expert(small[:, 6, 0:NT * GROUPS]), ALU.add))
            rank(sel, masked, EXPERTS, rank_a, rank_b, 0, NT, between=(4, 5, 6, 7))
            link(nc.vector.tensor_scalar(small[:, 5], small[:, 5], float(TOPK), None, ALU.is_lt))
            link(nc.vector.tensor_tensor(small[:, 5], small[:, 5], small[:, 2], ALU.mult))
            link(nc.vector.tensor_reduce(small[:, 7, 0:NT], sel, axis=X, op=ALU.add))
            link(nc.vector.reciprocal(small[:, 7, NT:2 * NT], small[:, 7, 0:NT]))
            link(nc.vector.tensor_scalar(small[:, 7, NT:2 * NT], small[:, 7, NT:2 * NT], 0.5, None, ALU.mult))
            link(nc.vector.tensor_tensor(sel, sel, small[:, 7, NT:2 * NT].rearrange("p (i o) -> p i o", o=1).to_broadcast([P, NT, EXPERTS]), ALU.mult))
            nc.vector.tensor_copy(cw_rep.rearrange("p i (e q) -> p (i e) q", q=Q),
                                  small[:, 5].rearrange("p (n o) -> p n o", o=1).to_broadcast([P, NT * EXPERTS, Q])).then_inc(s_cwrep, 1)
            dve.wait_ge(s_lam, 2)

            with dve.Fori(0, HALVES) as hf:
                u0 = hf * UNITS
                n0 = hf * STEPS

                def silu(k):
                    m = size_of(k)
                    dve.wait_ge(s_th, u0 + (k + 1 + CREDIT))
                    nc.vector.scalar_tensor_tensor(hid[0:m, k % 2], hid[0:m, k % 2], 1.0, bank(B_UP, rows=m), ALU.add, ALU.mult).then_inc(s_u, 1)

                def hidden(k):
                    m = size_of(k)
                    dve.wait_ge(s_b, u0 + (k + 1 + CREDIT))
                    if k < SHT:
                        dve.wait_ge(s_u, u0 + (k + 1 + CREDIT))
                        nc.vector.scalar_tensor_tensor(hid[0:m, k % 2], hid[0:m, k % 2], 0.5, bank(B_GATE, rows=m), ALU.mult, ALU.mult).then_inc(s_h, 1)
                    else:
                        dve.wait_ge(s_uc, hf * RTILES + (k - SHT + 2))
                        nc.vector.tensor_tensor(hid[0:m, k % 2], hid[0:m, k % 2], bank(B_GATE, rows=m), ALU.mult).then_inc(s_h, 1)

                def maxima(s, c):
                    i = ORDER[s % NT]
                    w = (i + 1) * P
                    at = (B_SCORE + (c if i < 4 else 0)) * BANK
                    dve.wait_ge(s_score, n0 * 2 + (2 * s + c + 1 + CREDIT + 2 * NT))
                    nc.vector.tensor_reduce(negmax[:, s % 4, c:c + 1], ps[:, at:at + w], axis=X, op=ALU.max, negate=True).then_inc(s_negmax, 1)

                def combine(s):
                    w = (ORDER[s % NT] + 1) * P
                    r2, cf = coef[:, s % 4, 0:1], coef[:, s % 4, 1:2]
                    dve.wait_ge(s_prob, n0 * 2 + (2 * s + 2 + CREDIT))
                    nc.vector.reciprocal(r2, sums[:, 1, bass.ds(hf, 1), s]).then_inc(s_chain, 1)
                    dve.wait_ge(s_chain, n0 * 2 + (2 * s + 1))
                    nc.vector.tensor_scalar(cf, r2, sums[:, 0, bass.ds(hf, 1), s], lam_t[:, 4:5], ALU.mult, ALU.mult).then_inc(s_chain, 1)
                    dve.wait_ge(s_chain, n0 * 2 + (2 * s + 2))
                    nc.vector.scalar_tensor_tensor(probs[:, s % 2, 0, 0:w], probs[:, s % 2, 1, 0:w], cf, probs[:, s % 2, 0, 0:w],
                                                   ALU.mult, ALU.add).then_inc(s_comb, 1)

                def copy_trans(s, grp):
                    gi = FIRST_GROUP[s] + grp
                    w = min(BANK, (ORDER[s % NT] + 1 - 4 * grp) * P)
                    dve.wait_ge(s_athi, hf * GPH + (gi + 1 + CREDIT))
                    nc.vector.tensor_tensor(at_lo[:, gi % 2, 0:w], ps[:, B_TRANS * BANK:B_TRANS * BANK + w],
                                            at_hi[:, gi % 2, 0:w].bitcast(F32), ALU.subtract).then_inc(s_atlo, 1)

                dve.wait_ge(s_vhi, hf + 1)
                nc.vector.tensor_tensor(v_lo[:, :, :], v_all[:, :, bass.ds(hf * P, P)], v_hi[:, :, :].bitcast(F32), ALU.subtract).then_inc(s_vlo, 1)
                for part, n in order["dve"]:
                    if part == "silu":
                        silu(n)
                    elif part == "hidden":
                        hidden(n)
                    elif part == "maxima":
                        maxima(*divmod(n, 2))
                    elif part == "combine":
                        combine(n)
                    elif part == "trans_lo":
                        copy_trans(*GROUP[n])
                dve.wait_ge(s_accth, hf + 1)
                nc.vector.scalar_tensor_tensor(gate[:, bass.ds(hf * 4, 4)].rearrange("p i e -> p (i e)"), probs[:, 0, 0], 1.0, bank(B_ACC, 2),
                                               ALU.add, ALU.mult).then_inc(s_accfree, 1)

            dve.wait_ge(s_w13lo, HALVES * UNITS + CREDIT)
            dve.wait_ge(s_w13hi, HALVES * UNITS + CREDIT)
            link(nc.vector.memset(head_ones, 0.0))
            for n in range(HH):
                last = nc.vector.memset(tail[n * DV:(n + 1) * DV, 10496 + n:10497 + n], 1.0 / DV)
            last.then_inc(s_fac, 1)
            l1 = sums[:, 0].rearrange("p f (h i) -> p f h i", i=NT)
            link(nc.vector.tensor_tensor(fac[:, 0], l1, l1, ALU.mult))
            for hf in range(HALVES):
                dve.wait_ge(s_ss, hf + 1)
                for pos, i in enumerate(ORDER):
                    src = ps[:, (4 + hf) * BANK + i * HH:(4 + hf) * BANK + (i + 1) * HH]
                    last = nc.vector.scalar_tensor_tensor(fac[:, 1, hf, :, pos], fac[:, 0, hf, :, pos], EPS, src, ALU.mult, ALU.add)
                last.then_inc(s_fac, 1)
                dve.wait_ge(s_sdf, hf + 1)
                link(nc.vector.reciprocal(fac[:, 2, hf], fac[:, 2, hf]))
                link(nc.vector.tensor_tensor(fac[:, 3, hf], fac[:, 2, hf], fac[:, 2, hf], ALU.mult))
                link(nc.vector.tensor_tensor(fac[:, 3, hf], fac[:, 3, hf], fac[:, 1, hf], ALU.mult))
                link(nc.vector.tensor_scalar(fac[:, 3, hf], fac[:, 3, hf], -0.5, 1.5, ALU.mult, ALU.add))
                link(nc.vector.tensor_tensor(fac[:, 2, hf], fac[:, 2, hf], fac[:, 3, hf], ALU.mult))
                for pos, i in enumerate(ORDER):
                    last = nc.vector.tensor_copy(frep[:, hf, i], fac[:, 2, hf, :, pos].rearrange("p (h o) -> p h o", o=1).to_broadcast([P, HH, DV]))
                last.then_inc(s_frep, 1)

            def norm_lo(hf):
                dve.wait_ge(s_onhi, hf + 1)
                nc.vector.tensor_tensor(xn_lo[:, hf], normed[:, hf], xn_hi[:, hf].bitcast(F32), ALU.subtract).then_inc(s_onlo, 1)

            for hf in range(HALVES):
                dve.wait_ge(s_fps, hf + 1)
                nc.vector.scalar_tensor_tensor(normed[:, hf], ot[:, hf], gcol[:, 1:2], bank(2 * hf, 2), ALU.mult, ALU.mult).then_inc(s_on, 1)
            norm_lo(0)
            norm_lo(1)
            dve.wait_ge(s_xre, 16)
            for r in range(4):
                two = slice(2 * r, 2 * r + 2)
                dve.wait_ge(s_so, r + 1)
                link(nc.vector.tensor_tensor(result[:, two], gate[:, two], bank(4 + r).rearrange("p (i e) -> p i e", e=E), ALU.mult))
                for i in (2 * r, 2 * r + 1):
                    nc.vector.scalar_tensor_tensor(result[:, i], result[:, i], 0.5, x_again[:, i], ALU.mult, ALU.add).then_inc(s_res, 1)

        @block.gpsimd
        def _(pool):
            links = [0]

            def link(ins):
                links[0] += 1
                ins.then_inc(s_link_p, 1)
                pool.wait_ge(s_link_p, links[0])

            for s in (s_w13lo, s_w2lo, s_hlo):
                pool.sem_inc(s, CREDIT)
            pool.sem_inc(s_uc, 1)
            link(pool.memset(ident[:, :], 0.0))
            pool.affine_select(out=ident[:, :], in_=ident[:, :], compare_op=ALU.not_equal, fill=1.0, base=0,
                               pattern=[[-1, P]], channel_multiplier=1).then_inc(s_const, 1)
            link(pool.memset(lower16[:, :, :], 1.0))
            link(pool.affine_select(out=lower16[:, :, :], in_=lower16[:, :, :], compare_op=ALU.is_ge, fill=0.0, base=-1,
                                    pattern=[[1, EXPERTS], [-1, EXPERTS]], channel_multiplier=0))
            link(pool.memset(ident_bf[:, :], 0.0))
            link(pool.affine_select(out=ident_bf[:, :], in_=ident_bf[:, :], compare_op=ALU.not_equal, fill=1.0, base=0,
                                    pattern=[[-1, P]], channel_multiplier=1))
            link(pool.memset(causal[:, :], 0.0))
            pool.affine_select(out=causal[:, :], in_=causal[:, :], compare_op=ALU.is_ge, fill=-BIG, base=0,
                               pattern=[[-1, P]], channel_multiplier=1).then_inc(s_const, 1)

            def split_lo(n):
                slot = (0, 1, 0, 1)[n]
                return pool.tensor_tensor(out=w_ring[:, slot, 1].rearrange("p m n -> p (m n)"), in0=wraw[:, n].rearrange("p k e -> p (k e)"),
                                          in1=w_ring[:, slot, 0].bitcast(F32).rearrange("p m n -> p (m n)"), op=ALU.subtract)

            for n in range(3):
                pool.wait_ge(s_phi, n + 1)
                if n == 2:
                    pool.wait_ge(s_proj, 4)
                split_lo(n).then_inc(s_plo, 1)
                for r in range(4 * n - 4, 4 * n):
                    if r >= 0:
                        pool.wait_ge(s_part1, r + 1)
                        at = slice(r % 2 * TH, (r % 2 + 1) * TH)
                        pool.tensor_tensor(out=stage[r // 2][:, 2, at], in0=resid[r % 4], in1=stage[r // 2][:, 1, at], op=ALU.subtract).then_inc(s_parts, 1)
            pool.wait_ge(s_v, 4)
            pool.wait_ge(s_cwb, 1)

            with pool.Fori(0, HALVES) as hf:
                u0 = hf * UNITS

                def split_w13(k):
                    pool.wait_ge(s_w13hi, u0 + (k + 1 + CREDIT))
                    pool.tensor_tensor(out=ring_tile(k, 1), in0=raw_tile(k), in1=ring_tile(k, 0, F32), op=ALU.subtract).then_inc(s_w13lo, 1)

                def split_w2(k):
                    m = size_of(k)
                    pool.wait_ge(s_w2hi, u0 + (k + 1 + CREDIT))
                    pool.tensor_tensor(out=w2_ring[0:m, k % 2, 1], in0=w2r[0:m, k], in1=w2_ring[0:m, k % 2, 0].bitcast(F32),
                                       op=ALU.subtract).then_inc(s_w2lo, 1)

                def hidden_lo(k):
                    m = size_of(k)
                    pool.wait_ge(s_hhi, u0 + (k + 1 + CREDIT))
                    pool.tensor_tensor(out=h_lo[0:m, k % 2], in0=hid[0:m, k % 2], in1=h_hi[0:m, k % 2].bitcast(F32), op=ALU.subtract).then_inc(s_hlo, 1)

                def weigh(k):
                    if k == SHT:
                        pool.wait_ge(s_cwhalf, hf + 1)
                    pool.wait_ge(s_u, u0 + (k + 1 + CREDIT))
                    pool.tensor_tensor(out=hid[:, k % 2], in0=hid[:, k % 2], in1=cw_half[:, :], op=ALU.mult).then_inc(s_uc, 1)

                for part, n in order["pool"]:
                    if part == "w13_lo":
                        split_w13(n)
                    elif part == "w2_lo":
                        split_w2(n)
                    elif part == "weigh":
                        weigh(n)
                    elif part == "hidden_lo":
                        hidden_lo(n)
            pool.wait_ge(s_wohi, 1)
            split_lo(3).then_inc(s_wolo, 1)


_INS = ["L0_attn_x", "L0_attn_Wq", "L0_attn_Wk", "L0_attn_Wv", "L0_attn_Wo", "L0_attn_lambda_q1", "L0_attn_lambda_k1",
        "L0_attn_lambda_q2", "L0_attn_lambda_k2", "L0_attn_g", "L0_ffn_gate_w", "L0_ffn_expert_bias", "L0_ffn_w1",
        "L0_ffn_w2", "L0_ffn_w3", "L0_ffn_sw1", "L0_ffn_sw2", "L0_ffn_sw3"]


def kernel(**inputs):
    import numpy as _np
    import concourse.bacc as _bacc
    from concourse.bass_utils import run_bass_kernel_spmd as _run

    nc = _bacc.Bacc("TRN2", target_bir_lowering=False, num_devices=1)
    arrays, args = {}, []
    for name in _INS:
        a = _np.ascontiguousarray(inputs[name])
        arrays[name] = a
        args.append(nc.dram_tensor(name, a.shape, mybir.dt.from_np(a.dtype), kind="ExternalInput").ap())
    out = nc.dram_tensor("out", (1, T, E), F32, kind="ExternalOutput").ap()
    build(nc, *args, out)
    r = _run(nc, [arrays], core_ids=[0])
    return r.results[0]["out"]
```

```python
import math
from contextlib import ExitStack

import numpy as np

import concourse.bass as bass
from concourse import mybir

F32 = mybir.dt.float32
F32R = mybir.dt.float32r
BF16 = mybir.dt.bfloat16
ALU = mybir.AluOpType
ACT = mybir.ActivationFunctionType
X = mybir.AxisListType.X

P = 128
BANK = 512
T = 1024
E = 256
NT = T // P
KH = E // P
HEADS = 8
D = 16
DV = 2 * D
HALVES = 2
TH = T // HALVES
HH = HEADS // HALVES
EXPERTS, GROUPS, TOPK, TOPG = 16, 4, 4, 2
PER_GROUP = EXPERTS // GROUPS
INTER = 176
SHARED = 2 * INTER
ROUTED = EXPERTS * INTER
Q = P // EXPERTS
RTILES = INTER // Q
SH_SIZES = [P, P, SHARED - 2 * P]
SHT = len(SH_SIZES)
UNITS = SHT + RTILES
LAMBDA_INIT = 0.8 - 0.6 * math.exp(-0.3 * 12)
EPS = 1e-5
BIG = 3.0e38

Q_PART = [0, 0, 1, 1, 0, 2]
K_PART = [0, 1, 0, 1, 2, 0]
STACK = len(Q_PART) * D
STACK_DMAS = 16 * 2 * len(Q_PART)

ORDER = [7, 0, 6, 1, 5, 2, 4, 3]
STEPS = HH * NT
GROUP_OF = [1 + (ORDER[s % NT] >= 4) for s in range(STEPS)]
FIRST_GROUP = [sum(GROUP_OF[:s]) for s in range(STEPS)]
GPH = sum(GROUP_OF)
GROUP = [(s, grp) for s in range(STEPS) for grp in range(GROUP_OF[s])]

PHASE = 4
PIECES = 6
UNIT_SHARE = [0.805, 0.883, 1.087, 0.864, 1.158, 0.916, 1.279, 1.007]
PIECE_SHARE = [2.5, 1.0, 1, 1, 1, 1]
LEAD = 8
ENDING = 12
NORM_AT = {"squares": 8, "square_sums": 8.5, "variance": 9, "deviation": 9.5, "factors": 10, "factors_back": 10.5, "normalise": 11}
TILE_AT = {"up_w1": 0, "up_w3": 1, "tanh": 0.5, "silu": 2, "weigh": 2.5, "hidden": 5,
           "hidden_hi": 6, "hidden_lo": 5, "w2_hi": 4, "w2_lo": 3, "w13_hi": -9, "w13_lo": -5,
           "down": 8, "v": 5, "spread": 5}
STEP_AT = {("scores", False): (0.5, 0.5), ("scores", True): (-0.5, 1.5),
           ("maxima", False): (1.003, 1.003), ("maxima", True): (-0.497, 2.502),
           ("exponentials", False): (1.502, 1.502), ("exponentials", True): (0.502, 2.502),
           ("reciprocal", False): 2.998, ("reciprocal", True): 4.498,
           ("coefficient", False): 3.999, ("coefficient", True): 4.499,
           ("combine", False): 4, ("combine", True): 4.5,
           ("transpose", False): (5.9999,), ("transpose", True): (5.9999, 7.9999),
           ("trans_hi", False): (6.5,), ("trans_hi", True): (6, 8.5),
           ("trans_lo", False): (7,), ("trans_lo", True): (7, 9.0001),
           ("values", False): (9.0001,), ("values", True): (9.0001, 11.0001),
           ("copy_out", False): 10.4, ("copy_out", True): 11.4}


def by_engine():
    tile = sum(PIECE_SHARE)
    lead = sum(PIECE_SHARE[:LEAD % PIECES]) + LEAD // PIECES * tile
    total = (UNITS + 1) * tile
    shares = [UNIT_SHARE[u % len(UNIT_SHARE)] for u in range(PHASE * (STEPS + 2))]
    marks = [0.0] + [lead + sum(shares[:u]) / sum(shares) * (total - lead) for u in range(len(shares) + 1)] + [total + 100.0]
    units = [-4.0] + list(range(len(shares) + 1)) + [len(shares) + 100.0]

    def at(piece):
        k, r = divmod(piece, PIECES)
        share = k * tile + sum(PIECE_SHARE[:int(r)]) + (r - int(r)) * PIECE_SHARE[int(r)]
        return float(np.interp(share, marks, units))

    order = {"pe": [], "act": [], "dve": [], "pool": []}
    latest = {}

    def place(engine, part, n, where):
        where = max(where, latest.get(part, where))
        latest[part] = where
        order[engine].append((where, part, n))

    for k in range(UNITS):
        for engine, part in (("pe", "up_w1"), ("pe", "up_w3"), ("act", "tanh"), ("dve", "silu"), ("pool", "weigh"), ("dve", "hidden"),
                             ("act", "hidden_hi"), ("pool", "hidden_lo"), ("act", "w2_hi"), ("pool", "w2_lo"), ("act", "w13_hi"),
                             ("pool", "w13_lo")):
            if k >= {"weigh": SHT, "w13_hi": 2, "w13_lo": 2}.get(part, 0):
                place(engine, part, k, at(PIECES * k + TILE_AT[part]))
        for i in range(TH // P):
            place("pe", "down", k * (TH // P) + i, at(PIECES * k + TILE_AT["down"] + i))
    place("act", "v_hi", 0, at(TILE_AT["v"]))
    place("dve", "v_lo", 0, at(TILE_AT["v"]))
    place("pe", "spread", 0, at(TILE_AT["spread"]))
    place("act", "spread_copy", 0, at(TILE_AT["spread"]))
    for s in range(STEPS):
        large = ORDER[s % NT] >= 4
        for engine, part in (("pe", "scores"), ("dve", "maxima"), ("act", "exponentials")):
            for c in range(2):
                place(engine, part, 2 * s + c, PHASE * s + STEP_AT[part, large][c])
        for part in ("reciprocal", "coefficient", "combine"):
            place("dve", part, s, PHASE * s + STEP_AT[part, large])
        for grp in range(GROUP_OF[s]):
            for engine, part in (("pe", "transpose"), ("act", "trans_hi"), ("dve", "trans_lo"), ("pe", "values")):
                place(engine, part, FIRST_GROUP[s] + grp, PHASE * s + STEP_AT[part, large][grp])
        place("act", "copy_out", s, PHASE * s + STEP_AT["copy_out", large])
    return {engine: [(part, n) for _, part, n in sorted(parts, key=lambda p: p[0])] for engine, parts in order.items()}


def size_of(k):
    return SH_SIZES[k] if k < SHT else P


B_ACC, B_UP, B_GATE, B_SCORE, B_TRANS, B_OUT = 0, 2, 3, 4, 6, 7
CREDIT = 2


def build(nc, x, wq, wk, wv, wo, lq1, lk1, lq2, lk2, g, gate_w, bias, w1, w2, w3, sw1, sw2, sw3, out):
    ctx = ExitStack()
    with ctx:
        def sb(name, shape, dt=F32):
            return ctx.enter_context(nc.sbuf_tensor(name, shape, dt))

        def sem(name):
            return ctx.enter_context(nc.semaphore(name))

        qk_parts = nc.dram_tensor("qk_parts", [2, 3, E, T], BF16, kind="Internal").ap()

        xn_hi = sb("xn_hi", [P, KH, T], F32R)
        xn_lo = sb("xn_lo", [P, KH, T], F32R)
        w13 = sb("w13", [P, 2 * KH, ROUTED + SHARED])
        w2r = sb("w2r", [P, UNITS, E])
        wraw = sb("wraw", [P, 4, KH, E])
        w_ring = sb("w_ring", [P, 2, 2, 2 * KH, P], F32R)
        w2_ring = sb("w2_ring", [P, 2, 2, E], F32R)
        v_all = sb("v_all", [P, NT, E])
        v_hi = sb("v_hi", [P, NT, P], F32R)
        v_lo = sb("v_lo", [P, NT, P], F32R)
        cw_rep = sb("cw_rep", [P, TH // P, P])
        cw_half = sb("cw_half", [P, TH])
        spare = sb("spare", [P, TH])
        qs = sb("qs", [P, 2, 2, T], BF16)
        ks = sb("ks", [P, 2, 2, T], BF16)
        probs = sb("probs", [P, 2, 2, T])
        at_hi = sb("at_hi", [P, 2, BANK], F32R)
        at_lo = sb("at_lo", [P, 2, BANK], F32R)
        hid = sb("hid", [P, 2, TH])
        h_hi = sb("h_hi", [P, 2, TH], F32R)
        h_lo = sb("h_lo", [P, 2, TH], F32R)
        ot = sb("ot", [P, HALVES, T])
        gate = sb("gate", [P, NT, E])
        ident = sb("ident", [P, P])
        ident_bf = sb("ident_bf", [P, P], BF16)
        causal = sb("causal", [P, P], BF16)
        lower16 = sb("lower16", [P, EXPERTS, EXPERTS])
        negmax = sb("negmax", [P, 4, 2])
        coef = sb("coef", [P, 4, 2])
        sums = sb("sums", [P, 2, HALVES, STEPS])
        gcol = sb("gcol", [P, 2])
        gw_raw = sb("gw_raw", [EXPERTS, E])
        gwt = sb("gwt", [P, 2, KH, EXPERTS], F32R)
        bias_b = sb("bias_b", [P, EXPERTS])
        lams = sb("lams", [P, 4, D])
        lam_t = sb("lam_t", [P, 8])
        stats = sb("stats", [P, NT, 6])
        mv = sb("mv", [P, NT, 2])
        ln_t = sb("ln_t", [P, 4, NT])

        ps = ctx.enter_context(nc.psum_tensor("ps", [P, 8 * BANK], F32))

        def bank(b, n=1, rows=P):
            return ps[0:rows, b * BANK:(b + n) * BANK]

        small = wraw[:, 0:2].rearrange("p n k e -> p (n k e)").rearrange("p (n t) -> p n t", n=8)
        xt = probs[:, 0].rearrange("p c (i e) -> p (c i) e", e=E)
        rank_a = probs[:, 0, 0].bitcast(BF16)
        rank_b = probs[:, 0, 1].bitcast(BF16)
        resid = [cw_rep[:, :, :].rearrange("p i r -> p (i r)"), spare[:, :], cw_half[:, :], hid[:, 1]]
        lg_t = hid[:, 0]
        stage = [t[:, 0:3 * T].rearrange("p (a t) -> p a t", a=3) for t in
                 (ot[:, :, :].rearrange("p a b -> p (a b)").bitcast(BF16), gate[:, :, :].rearrange("p a b -> p (a b)").bitcast(BF16),
                  probs[:, 1].rearrange("p a b -> p (a b)").bitcast(BF16), qs[:, :, :, :].rearrange("p a c t -> p (a c t)"))]
        sel_g = small[:, 0, 0:NT * GROUPS].rearrange("p (i a) -> p i a", a=GROUPS)

        def table(n):
            return small[:, n].rearrange("p (i e) -> p i e", e=EXPERTS)

        s_x1, s_wqkv, s_gatew, s_vecs, s_sh, s_w13, s_w2, s_wo = map(
            sem, ["x_in", "wqkv_in", "gate_in", "vecs_in", "shared_in", "w13_in", "w2_in", "wo_in"])
        s_x = [s_x1, sem("x_in_2")]
        s_const = sem("const_made")
        s_link_v, s_link_p = sem("vector_link"), sem("pool_link")
        s_var, s_std, s_xn, s_xt, s_xhi, s_xlo = map(
            sem, ["var_ready", "std_ready", "xn_ready", "xn_transposed", "xn_hi_ready", "xn_lo_ready"])
        s_gwt_ps, s_gwt_hi, s_gwt = sem("gate_transposed"), sem("gate_hi_ready"), sem("gate_parts_ready")
        s_phi, s_plo = sem("proj_hi_ready"), sem("proj_lo_ready")
        s_proj, s_part0, s_resid, s_part1, s_parts = map(sem, ["proj_done", "part0_ready", "resid_ready", "part1_ready", "parts_ready"])
        s_stored = [sem(f"parts_stored_{n}") for n in range(4)]
        s_v = sem("v_ready")
        s_lgt, s_lgc, s_lg, s_el, s_cwrep, s_cwt = map(
            sem, ["logits_t_done", "logits_t_copied", "logits_done", "exp_logits_ready", "weights_ready",
                  "weights_transposed"])
        s_dot, s_edot, s_lam = sem("lambda_dots"), sem("lambda_exps"), sem("lambda_ready")

        s_w13hi, s_w13lo, s_w2hi, s_w2lo = map(sem, ["w13_hi_split", "w13_lo_split", "w2_hi_split", "w2_lo_split"])
        s_a, s_b, s_th, s_u, s_uc, s_h, s_hhi, s_hlo, s_down = map(
            sem, ["w1_product", "w3_product", "tanh_ready", "silu_ready", "weighted_ready", "hidden_ready",
                  "hidden_hi", "hidden_lo", "down_done"])
        s_accth, s_accfree = sem("acc_tanh"), sem("acc_free")
        s_stack = [sem(f"stacks_in_{n}") for n in range(2)]
        s_score, s_negmax, s_prob, s_rsum, s_coef, s_comb = map(
            sem, ["scores_done", "negmax_ready", "probs_ready", "sum_reciprocal", "coefficient", "combined"])
        s_trans, s_athi, s_atlo, s_pv, s_oev = map(
            sem, ["transposed", "trans_hi", "trans_lo", "pv_done", "out_copied"])
        s_vhi, s_vlo = sem("v_hi_split"), sem("v_lo_split")
        s_cwhalf = sem("weights_of_half")
        s_xre, s_sq, s_ss, s_fac, s_sdf, s_frep, s_fps, s_on, s_onhi, s_onlo, s_wohi, s_wolo, s_so, s_gated, s_res_v, s_res_p, s_out = map(
            sem, ["x_again", "squares", "sum_squares", "var_of_heads", "std_of_heads", "factors", "factors_t",
                  "normed", "normed_hi", "normed_lo", "wo_hi", "wo_lo", "attn_out", "gated", "result_of_vector", "result_of_pool", "stored"])

        tail = w13[:, :, :].rearrange("p a b -> p (a b)")
        x_again = tail[:, 0:NT * E].rearrange("p (i e) -> p i e", e=E)
        squares = tail[:, 2048:4096].rearrange("p (a t) -> p a t", a=HALVES)
        frep = tail[:, 4096:6144].rearrange("p (a i h r) -> p a i h r", a=HALVES, h=HH, r=DV)
        normed = tail[:, 6144:8192].rearrange("p (a t) -> p a t", a=HALVES)
        result = tail[:, 8192:10240].rearrange("p (i e) -> p i e", e=E)
        fac = tail[:, 10240:10240 + 4 * NT * HEADS].rearrange("p (n a h i) -> p n a h i", n=4, a=HALVES, i=NT)
        head_ones = tail[:, 10496:10500]

        def three(pe_out, a_hi, a_lo, b_hi, b_lo, first, last, skip=False):
            nc.tensor.matmul(pe_out, a_hi, b_hi, start=first, stop=False, skip_group_check=skip)
            nc.tensor.matmul(pe_out, a_hi, b_lo, start=False, stop=False, skip_group_check=skip)
            return nc.tensor.matmul(pe_out, a_lo, b_hi, start=False, stop=last, skip_group_check=skip)

        def proj_w(slot, part, kh):
            return w_ring[:, slot, part].rearrange("p m n -> p (m n)")[:, kh * E:(kh + 1) * E]

        def raw_tile(k):
            if k < SHT:
                return w13[:, :, ROUTED + k * P:ROUTED + k * P + size_of(k)]
            return w13[:, :, 0:ROUTED].rearrange("p m (e h) -> p m e h", h=INTER)[:, :, :, (k - SHT) * Q:(k - SHT + 1) * Q]

        def ring_tile(k, part, dt=None):
            t = w_ring[:, k % 2, part, :, 0:size_of(k)]
            t = t if dt is None else t.bitcast(dt)
            return t if k < SHT else t.rearrange("p m (e q) -> p m e q", q=Q)

        order = by_engine()

        block = ctx.enter_context(nc.Block())

        @block.sync
        def _(sp):
            xv = x.rearrange("o (i p) e -> p (o i) e", p=P)
            for half in range(2):
                sp.dma_start(xt[:, half * 4:half * 4 + 4], xv[:, half * 4:half * 4 + 4]).then_inc(s_x[half], 16)
            sp.dma_start(gw_raw[:, :], gate_w).then_inc(s_gatew, 16)
            for n, w in enumerate((wq, wk, wv)):
                sp.dma_start(wraw[:, n], w.rearrange("(k p) e -> p k e", p=P)).then_inc(s_wqkv, 16)
            for n, v in enumerate((lq1, lk1, lq2, lk2)):
                sp.dma_start(lams[:, n], v.rearrange("(o d) -> o d", o=1).to_broadcast([P, D])).then_inc(s_vecs, 16)
            sp.dma_start(bias_b[:, :], bias.rearrange("(o d) -> o d", o=1).to_broadcast([P, EXPERTS])).then_inc(s_vecs, 16)
            for n in range(HH):
                sp.dma_start(gcol[n * DV:(n + 1) * DV, 0:1], g.rearrange("(d o) -> d o", o=1)).then_inc(s_vecs, 16)
            for m, w in enumerate((sw1, sw3)):
                sp.dma_start(w13[:, m * KH:(m + 1) * KH, ROUTED:], w.rearrange("(k p) h -> p k h", p=P)).then_inc(s_sh, 16)
            sp.dma_start(w2r[:, 0:2, :], sw2[0:2 * P].rearrange("(s p) e -> p s e", p=P)).then_inc(s_sh, 16)
            sp.dma_start(w2r[0:SH_SIZES[2], 2, :], sw2[2 * P:]).then_inc(s_sh, 16)

            def load_w13(m, kh):
                sp.dma_start(w13[:, m * KH + kh, 0:ROUTED].rearrange("p (e h) -> p e h", h=INTER),
                             (w1, w3)[m][:, kh * P:(kh + 1) * P, :].rearrange("e p h -> p e h")).then_inc(s_w13, 16)

            load_w13(0, 0)
            load_w13(0, 1)
            load_w13(1, 0)
            for n in range(4):
                sp.wait_ge(s_parts, 2 * n + 2)
                sp.dma_start(qk_parts[n // 2, :, (n % 2) * P:(n % 2 + 1) * P, :].rearrange("a p t -> p a t"), stage[n]).then_inc(s_stored[n], 16)
                for e in range(EXPERTS // 2) if n == 0 else range(EXPERTS // 2, EXPERTS) if n == 3 else ():
                    sp.dma_start(w2r[e * Q:(e + 1) * Q, SHT:, :], w2[e].rearrange("(j q) d -> q j d", q=Q)).then_inc(s_w2, 16)
            load_w13(1, 1)
            for n in range(4):
                sp.wait_ge(s_stored[n], 16)
            rows = qk_parts.rearrange("s a (f h c d) t -> (s a f h) d c t", f=HALVES, h=HH, c=2)
            with sp.Fori(0, HALVES) as hf:
                for a in range(HH):
                    sp.wait_ge(s_score, hf * (2 * STEPS) + (2 * NT * (a - 1) + CREDIT + 2 * NT))
                    for n in range(2):
                        stack = (qs, ks)[n]
                        for r, part in enumerate((Q_PART, K_PART)[n]):
                            row = ((n * 3 + part) * HALVES) * HH + a
                            sp.dma_start(stack[r * D:(r + 1) * D, a % 2],
                                         rows[bass.ds(hf * HH + row, 1)].rearrange("o d c t -> (o d) c t")).then_inc(s_stack[a % 2], 16)
            sp.dma_start(wraw[:, 3], wo.rearrange("(k p) e -> p k e", p=P)).then_inc(s_wo, 16)
            sp.wait_ge(s_fac, 1)
            sp.dma_start(x_again, xv).then_inc(s_xre, 16)
            for r in range(NT // 2):
                sp.wait_ge((s_res_p, s_res_v)[r % 2], r // 2 + 1)
                sp.dma_start(out.rearrange("o (i p) e -> p (o i) e", p=P)[:, 2 * r:2 * r + 2], result[:, 2 * r:2 * r + 2]).then_inc(s_out, 16)
            sp.wait_ge(s_out, 16 * (NT // 2))

        @block.tensor
        def _(pe):
            pe.sem_inc(s_a, CREDIT)
            pe.sem_inc(s_b, CREDIT)
            pe.sem_inc(s_down, CREDIT)
            pe.sem_inc(s_trans, 1)
            pe.sem_inc(s_pv, CREDIT)
            pe.sem_inc(s_score, CREDIT + 2 * NT)
            pe.wait_ge(s_const, 1)
            pe.wait_ge(s_gatew, 16)
            for kh in range(KH):
                last = nc.tensor.transpose(ps[:, 3 * BANK + kh * EXPERTS:3 * BANK + (kh + 1) * EXPERTS],
                                           gw_raw[:, kh * P:(kh + 1) * P], ident[0:EXPERTS, 0:EXPERTS])
            last.then_inc(s_gwt_ps, 1)
            for i in range(NT):
                pe.wait_ge(s_xn, i + 1)
                for kh in range(KH):
                    b = 4 + 2 * (i // 4) + kh
                    last = nc.tensor.transpose(ps[:, b * BANK + (i % 4) * P:b * BANK + (i % 4 + 1) * P],
                                               xt[:, i, kh * P:(kh + 1) * P], ident[:, :])
                last.then_inc(s_xt, 1)
            for r in range(8):
                n, mt, c = r // 4, (r // 2) % 2, r % 2
                if r < 2:
                    pe.wait_ge(s_xhi, 2 * c + 2)
                    pe.wait_ge(s_xlo, 2 * c + 2)
                if r == 3:
                    pe.wait_ge(s_gwt, 1)
                if r % 4 == 0:
                    pe.wait_ge(s_phi, n + 1)
                    pe.wait_ge(s_plo, n + 1)
                if r >= 4:
                    pe.wait_ge(s_resid, r - 3)
                for kh in range(KH):
                    last = three(bank(r % 4), proj_w(n, 0, kh)[:, mt * P:(mt + 1) * P], proj_w(n, 1, kh)[:, mt * P:(mt + 1) * P],
                                 xn_hi[:, kh, c * TH:(c + 1) * TH], xn_lo[:, kh, c * TH:(c + 1) * TH], kh == 0, kh == KH - 1)
                last.then_inc(s_proj, 1)
                if r == 1:
                    pe.wait_ge(s_gwt, 1)
                    for half in range(2):
                        for kh in range(KH):
                            last = three(bank(4 + half, rows=EXPERTS), gwt[:, 0, kh], gwt[:, 1, kh], xn_hi[:, kh, half * TH:(half + 1) * TH],
                                         xn_lo[:, kh, half * TH:(half + 1) * TH], kh == 0, kh == KH - 1)
                        last.then_inc(s_lgt, 1)
                if r == 2:
                    for i in range(NT):
                        if i % 4 == 0:
                            pe.wait_ge(s_lgc, i // 4 + 1)
                        at = (6 + i // 4) * BANK + (i % 4) * EXPERTS
                        last = nc.tensor.transpose(ps[:, at:at + EXPERTS],
                                                   lg_t[32 * (i // 4):32 * (i // 4) + EXPERTS, (i % 4) * P:(i % 4 + 1) * P],
                                                   ident[32 * (i // 4):32 * (i // 4) + EXPERTS, 32 * (i // 4):32 * (i // 4) + EXPERTS])
                    last.then_inc(s_lg, 1)
            for r in range(8, 12):
                if r == 8:
                    pe.wait_ge(s_phi, 3)
                    pe.wait_ge(s_plo, 3)
                pe.wait_ge(s_resid, r - 3)
                for i in (2 * (r - 8), 2 * (r - 8) + 1):
                    for kh in range(KH):
                        last = three(ps[:, (r % 4) * BANK + (i % 2) * E:(r % 4) * BANK + (i % 2 + 1) * E],
                                     xn_hi[:, kh, i * P:(i + 1) * P], xn_lo[:, kh, i * P:(i + 1) * P],
                                     proj_w(0, 0, kh), proj_w(0, 1, kh), kh == 0, kh == KH - 1)
                last.then_inc(s_proj, 1)
            pe.wait_ge(s_v, 4)
            pe.wait_ge(s_el, 1)

            with pe.Fori(0, HALVES) as hf:
                u0 = hf * UNITS
                n0 = hf * STEPS

                def up(k, m13):
                    m = size_of(k)
                    if m13 == 0:
                        pe.wait_ge(s_w13hi, u0 + (k + 1 + CREDIT))
                        pe.wait_ge(s_w13lo, u0 + (k + 1 + CREDIT))
                        pe.wait_ge(s_u, u0 + (k + CREDIT))
                    else:
                        pe.wait_ge(s_h, u0 + (k + CREDIT))
                    for kh in range(KH):
                        last = three(bank(B_UP + m13, rows=m), w_ring[:, k % 2, 0, m13 * KH + kh, 0:m],
                                     w_ring[:, k % 2, 1, m13 * KH + kh, 0:m], xn_hi[:, kh, bass.ds(hf * TH, TH)],
                                     xn_lo[:, kh, bass.ds(hf * TH, TH)], kh == 0, kh == KH - 1)
                    last.then_inc((s_a, s_b)[m13], 1)

                def down(k, i):
                    m = size_of(k)
                    if i == 0:
                        pe.wait_ge(s_hhi, u0 + (k + 1 + CREDIT))
                        pe.wait_ge(s_hlo, u0 + (k + 1 + CREDIT))
                        pe.wait_ge(s_w2hi, u0 + (k + 1 + CREDIT))
                        pe.wait_ge(s_w2lo, u0 + (k + 1 + CREDIT))
                        if k == 0:
                            pe.wait_ge(s_accfree, hf + 1)
                    at = B_ACC * BANK + i * E
                    last = three(ps[:, at:at + E], h_hi[0:m, k % 2, i * P:(i + 1) * P], h_lo[0:m, k % 2, i * P:(i + 1) * P],
                                 w2_ring[0:m, k % 2, 0], w2_ring[0:m, k % 2, 1], k == 0 and i % 2 == 0, k == UNITS - 1, skip=True)
                    if i == TH // P - 1:
                        last.then_inc(s_down, 1)

                def scores(s, c):
                    a, i = s // NT, ORDER[s % NT]
                    if c == 0 and s % NT == 0:
                        pe.wait_ge(s_stack[a % 2], hf * (HH // 2 * STACK_DMAS) + STACK_DMAS * (a // 2 + 1))
                    behind = 1 if (i < 4 and c == 1) else 0
                    pe.wait_ge(s_prob, n0 * 2 + (2 * s + c - behind + CREDIT))
                    w = (i + 1) * P
                    q = qs[0:STACK, a % 2, c, i * P:(i + 1) * P]
                    at = (B_SCORE + (c if i < 4 else 0)) * BANK
                    for lo in range(0, w, BANK):
                        hi = min(lo + BANK, w)
                        diagonal = hi == w
                        nc.tensor.matmul(ps[:, at + lo:at + hi], q, ks[0:STACK, a % 2, c, lo:hi], start=True, stop=not diagonal)
                        if diagonal:
                            last = nc.tensor.matmul(ps[:, at + w - P:at + w], ident_bf[:, :], causal[:, :], start=False, stop=True)
                    last.then_inc(s_score, 1)

                def transposes(s, grp):
                    i = ORDER[s % NT]
                    gi = FIRST_GROUP[s] + grp
                    if grp == 0:
                        pe.wait_ge(s_comb, n0 + (s + 1 + CREDIT))
                    pe.wait_ge(s_atlo, hf * GPH + (gi + CREDIT))
                    for j in range(4 * grp, min(4 * grp + 4, i + 1)):
                        last = nc.tensor.transpose(ps[:, B_TRANS * BANK + (j % 4) * P:B_TRANS * BANK + (j % 4 + 1) * P],
                                                   probs[:, s % 2, 0, j * P:(j + 1) * P], ident[:, :])
                    last.then_inc(s_trans, 1)

                def values(s, grp):
                    a, i = s // NT, ORDER[s % NT]
                    gi = FIRST_GROUP[s] + grp
                    if s == 0 and grp == 0:
                        pe.wait_ge(s_vhi, hf + 1)
                        pe.wait_ge(s_vlo, hf + 1)
                    if grp == 0:
                        pe.wait_ge(s_oev, n0 + (s + CREDIT))
                    pe.wait_ge(s_athi, hf * GPH + (gi + 1 + CREDIT))
                    pe.wait_ge(s_atlo, hf * GPH + (gi + 1 + CREDIT))
                    for j in range(4 * grp, min(4 * grp + 4, i + 1)):
                        last = three(ps[0:DV, B_OUT * BANK:B_OUT * BANK + P], v_hi[:, j, a * DV:(a + 1) * DV], v_lo[:, j, a * DV:(a + 1) * DV],
                                     at_hi[:, gi % 2, (j % 4) * P:(j % 4 + 1) * P], at_lo[:, gi % 2, (j % 4) * P:(j % 4 + 1) * P],
                                     j == 0, j == i)
                    last.then_inc(s_pv, 1)

                def spread_weights():
                    pe.wait_ge(s_cwrep, hf + 1)
                    pe.wait_ge(s_atlo, hf * GPH + CREDIT)
                    for i in range(TH // P):
                        last = nc.tensor.transpose(ps[:, B_TRANS * BANK + i * P:B_TRANS * BANK + (i + 1) * P], cw_rep[:, i], ident[:, :])
                    last.then_inc(s_cwt, 1)
                    pe.wait_ge(s_cwhalf, hf + 1)

                for part, n in order["pe"]:
                    if part == "up_w1":
                        up(n, 0)
                    elif part == "up_w3":
                        up(n, 1)
                    elif part == "down":
                        down(*divmod(n, TH // P))
                    elif part == "scores":
                        scores(*divmod(n, 2))
                    elif part == "spread":
                        spread_weights()
                    elif part == "transpose":
                        transposes(*GROUP[n])
                    elif part == "values":
                        values(*GROUP[n])

            for hf in range(HALVES):
                pe.wait_ge(s_sq, hf + 1)
                pe.wait_ge(s_fac, 1)
                for i in range(NT):
                    at = (4 + hf) * BANK + i * HH
                    last = nc.tensor.matmul(ps[:, at:at + HH], squares[:, hf, i * P:(i + 1) * P], head_ones, start=True, stop=True)
                last.then_inc(s_ss, 1)
            pe.wait_ge(s_accfree, 3)
            for hf in range(HALVES):
                pe.wait_ge(s_frep, hf + 1)
                for i in range(NT):
                    at = 2 * hf * BANK + i * P
                    last = nc.tensor.transpose(ps[:, at:at + P], frep[:, hf, i].rearrange("p h r -> p (h r)"), ident[:, :])
                last.then_inc(s_fps, 1)
            pe.wait_ge(s_wohi, 1)
            pe.wait_ge(s_wolo, 1)
            pe.wait_ge(s_fac, 1 + HALVES)
            for kh in range(KH):
                pe.wait_ge(s_onhi, kh + 1)
                pe.wait_ge(s_onlo, kh + 1)
                for i in range(NT):
                    b = 4 + i // 2
                    last = three(ps[:, b * BANK + (i % 2) * E:b * BANK + (i % 2 + 1) * E],
                                 xn_hi[:, kh, i * P:(i + 1) * P], xn_lo[:, kh, i * P:(i + 1) * P],
                                 proj_w(1, 0, kh), proj_w(1, 1, kh), kh == 0 and i % 2 == 0, kh == KH - 1, skip=True)
                    if kh == KH - 1 and i % 2 == 1:
                        last.then_inc(s_so, 1)

        @block.scalar
        def _(act):
            for s in (s_w13hi, s_w2hi, s_th, s_hhi, s_prob, s_athi, s_oev):
                act.sem_inc(s, CREDIT)

            def split_hi(n):
                slot = (0, 1, 0, 1)[n]
                return nc.scalar.activation(w_ring[:, slot, 0].rearrange("p m n -> p (m n)"),
                                            wraw[:, n].rearrange("p k e -> p (k e)"), ACT.Copy)

            act.wait_ge(s_var, 1)
            nc.scalar.activation(ln_t[:, 1], ln_t[:, 0], ACT.Sqrt).then_inc(s_std, 1)
            act.wait_ge(s_gwt_ps, 1)
            nc.scalar.activation(gwt[:, 0].rearrange("p k e -> p (k e)"), ps[:, 3 * BANK:3 * BANK + KH * EXPERTS], ACT.Copy).then_inc(s_gwt_hi, 1)
            act.wait_ge(s_wqkv, 48)
            split_hi(0).then_inc(s_phi, 1)
            split_hi(1).then_inc(s_phi, 1)
            act.wait_ge(s_dot, 1)
            nc.scalar.activation(lam_t[:, 2:4], lam_t[:, 0:2], ACT.Exp).then_inc(s_edot, 1)
            for c in range(2):
                act.wait_ge(s_xt, 4 * c + 4)
                for kh in range(KH):
                    nc.scalar.activation(xn_hi[:, kh, c * TH:(c + 1) * TH], bank(4 + 2 * c + kh), ACT.Copy).then_inc(s_xhi, 1)
            def part_0(r):
                act.wait_ge(s_proj, r + 1)
                nc.scalar.activation(stage[r // 2][:, 0, r % 2 * TH:(r % 2 + 1) * TH], bank(r % 4), ACT.Copy,
                                     scale=D ** -0.5 if r < 4 else 1.0).then_inc(s_part0, 1)

            def part_1(r):
                act.wait_ge(s_resid, r + 1)
                nc.scalar.activation(stage[r // 2][:, 1, r % 2 * TH:(r % 2 + 1) * TH], resid[r % 4], ACT.Copy).then_inc(s_part1, 1)

            part_0(0)
            part_0(1)
            part_1(0)
            part_1(1)
            for c in range(2):
                act.wait_ge(s_lgt, c + 1)
                nc.scalar.activation(lg_t[32 * c:32 * c + EXPERTS, :], bank(4 + c, rows=EXPERTS), ACT.Copy).then_inc(s_lgc, 1)
            part_0(2)
            act.wait_ge(s_plo, 2)
            act.wait_ge(s_lg, 1)
            nc.scalar.activation(small[:, 1].rearrange("p (b n) -> p b n", b=2), bank(6, 2).rearrange("p (b n) -> p b n", b=2)[:, :, 0:4 * EXPERTS],
                                 ACT.Exp, scale=-1.0).then_inc(s_el, 1)
            for r in range(3, 9):
                if r < 8:
                    part_0(r)
                part_1(r - 1)
                if r == 4:
                    split_hi(2).then_inc(s_phi, 1)
            for r in range(4):
                act.wait_ge(s_proj, 9 + r)
                nc.scalar.activation(v_all[:, 2 * r:2 * r + 2].rearrange("p i e -> p (i e)"), bank(r % 4), ACT.Copy).then_inc(s_v, 1)
            act.wait_ge(s_v, 4)
            act.wait_ge(s_parts, 8)

            def split_w13(k):
                nc.scalar.activation(ring_tile(k, 0), raw_tile(k), ACT.Copy).then_inc(s_w13hi, 1)

            act.wait_ge(s_sh, 64)
            split_w13(0)
            split_w13(1)

            with act.Fori(0, HALVES) as hf:
                u0 = hf * UNITS
                n0 = hf * STEPS

                def split_w2(k):
                    m = size_of(k)
                    if k == SHT:
                        act.wait_ge(s_w2, 256)
                    act.wait_ge(s_down, u0 + (k + 1))
                    nc.scalar.activation(w2_ring[0:m, k % 2, 0], w2r[0:m, k], ACT.Copy).then_inc(s_w2hi, 1)

                def high_hidden(k):
                    m = size_of(k)
                    act.wait_ge(s_h, u0 + (k + 1 + CREDIT))
                    act.wait_ge(s_down, u0 + (k + 1))
                    nc.scalar.activation(h_hi[0:m, k % 2], hid[0:m, k % 2], ACT.Copy).then_inc(s_hhi, 1)

                def tanh(k):
                    m = size_of(k)
                    act.wait_ge(s_a, u0 + (k + 1 + CREDIT))
                    act.wait_ge(s_hlo, u0 + (k - 1 + CREDIT))
                    nc.scalar.activation(hid[0:m, k % 2], bank(B_UP, rows=m), ACT.Tanh, scale=0.5).then_inc(s_th, 1)

                def exponentials(s, c):
                    i = ORDER[s % NT]
                    w = (i + 1) * P
                    at = (B_SCORE + (c if i < 4 else 0)) * BANK
                    act.wait_ge(s_negmax, n0 * 2 + (2 * s + c + 1))
                    if c == 0:
                        act.wait_ge(s_trans, hf * GPH + (FIRST_GROUP[s - 1] + 1 if s else 1 - 0))
                    nc.scalar.activation(probs[:, s % 2, c, 0:w], ps[:, at:at + w], ACT.Exp, bias=negmax[:, s % 4, c:c + 1],
                                         accum_out=sums[:, c, bass.ds(hf, 1), s]).then_inc(s_prob, 1)

                def copy_trans(s, grp):
                    gi = FIRST_GROUP[s] + grp
                    w = min(BANK, (ORDER[s % NT] + 1 - 4 * grp) * P)
                    act.wait_ge(s_trans, hf * GPH + (gi + 2))
                    act.wait_ge(s_pv, hf * GPH + (gi + 1))
                    nc.scalar.activation(at_hi[:, gi % 2, 0:w], ps[:, B_TRANS * BANK:B_TRANS * BANK + w], ACT.Copy).then_inc(s_athi, 1)

                def copy_out(s):
                    a, i = s // NT, ORDER[s % NT]
                    act.wait_ge(s_pv, hf * GPH + (FIRST_GROUP[s] + GROUP_OF[s] + CREDIT))
                    nc.scalar.activation(ot[a * DV:(a + 1) * DV, bass.ds(hf, 1), i * P:(i + 1) * P].rearrange("p o t -> p (o t)"),
                                         ps[0:DV, B_OUT * BANK:B_OUT * BANK + P], ACT.Copy).then_inc(s_oev, 1)

                def high_values():
                    act.wait_ge(s_pv, hf * GPH + CREDIT)
                    nc.scalar.activation(v_hi[:, :, :], v_all[:, :, bass.ds(hf * P, P)], ACT.Copy).then_inc(s_vhi, 1)

                def copy_weights():
                    act.wait_ge(s_cwt, hf + 1)
                    act.wait_ge(s_uc, hf * RTILES + 1)
                    nc.scalar.activation(cw_half[:, :], bank(B_TRANS), ACT.Copy).then_inc(s_cwhalf, 1)

                for part, n in order["act"]:
                    if part == "w13_hi":
                        if n == SHT:
                            act.wait_ge(s_w13, 64)
                        act.wait_ge(s_b, u0 + (n + 1))
                        split_w13(n)
                    elif part == "w2_hi":
                        split_w2(n)
                    elif part == "v_hi":
                        high_values()
                    elif part == "spread_copy":
                        copy_weights()
                    elif part == "tanh":
                        tanh(n)
                    elif part == "hidden_hi":
                        high_hidden(n)
                    elif part == "exponentials":
                        exponentials(*divmod(n, 2))
                    elif part == "trans_hi":
                        copy_trans(*GROUP[n])
                    elif part == "copy_out":
                        copy_out(n)
                act.wait_ge(s_b, u0 + (UNITS + CREDIT))
                split_w13(0)
                split_w13(1)
                act.wait_ge(s_down, u0 + (UNITS + CREDIT))
                act.wait_ge(s_trans, hf * GPH + (GPH + 1))
                nc.scalar.activation(probs[:, 0, 0], bank(B_ACC, 2), ACT.Tanh, scale=0.5).then_inc(s_accth, 1)

            act.wait_ge(s_oev, HALVES * STEPS + CREDIT)
            act.wait_ge(s_w13hi, HALVES * UNITS + 2 + CREDIT)
            act.wait_ge(s_w13lo, HALVES * UNITS + 2 + CREDIT)
            for hf in range(HALVES):
                nc.scalar.activation(squares[:, hf], ot[:, hf], ACT.Square).then_inc(s_sq, 1)
            act.wait_ge(s_wo, 16)
            act.wait_ge(s_b, HALVES * UNITS + CREDIT)
            split_hi(3).then_inc(s_wohi, 1)
            for hf in range(HALVES):
                act.wait_ge(s_fac, 2 + hf)
                nc.scalar.activation(fac[:, 2, hf], fac[:, 1, hf], ACT.Sqrt).then_inc(s_sdf, 1)
            for hf in range(HALVES):
                act.wait_ge(s_on, hf + 1)
                nc.scalar.activation(xn_hi[:, hf], normed[:, hf], ACT.Copy).then_inc(s_onhi, 1)

        @block.vector
        def _(dve):
            links = [0]

            def link(ins):
                links[0] += 1
                ins.then_inc(s_link_v, 1)
                dve.wait_ge(s_link_v, links[0])

            for s in (s_u, s_h, s_comb, s_atlo):
                dve.sem_inc(s, CREDIT)
            dve.sem_inc(s_accfree, 1)
            for i in range(NT):
                if i % 4 == 0:
                    dve.wait_ge(s_x[i // 4], 16)
                last = nc.vector.bn_stats(stats[:, i], xt[:, i])
            link(last)
            for i in range(NT):
                last = nc.vector.bn_aggr(mv[:, i], stats[:, i])
            link(last)
            nc.vector.tensor_scalar(ln_t[:, 0], mv[:, :, 1], EPS, None, ALU.add).then_inc(s_var, 1)
            dve.wait_ge(s_std, 1)
            link(nc.vector.reciprocal(ln_t[:, 1], ln_t[:, 1]))
            link(nc.vector.tensor_tensor(ln_t[:, 2], ln_t[:, 1], ln_t[:, 1], ALU.mult))
            link(nc.vector.tensor_tensor(ln_t[:, 2], ln_t[:, 2], ln_t[:, 0], ALU.mult))
            link(nc.vector.tensor_scalar(ln_t[:, 2], ln_t[:, 2], -0.5, 1.5, ALU.mult, ALU.add))
            link(nc.vector.tensor_tensor(ln_t[:, 1], ln_t[:, 1], ln_t[:, 2], ALU.mult))
            for i in range(NT):
                nc.vector.tensor_scalar(xt[:, i], xt[:, i], mv[:, i, 0:1], ln_t[:, 1, i:i + 1], ALU.subtract, ALU.mult).then_inc(s_xn, 1)
            dve.wait_ge(s_vecs, 144)
            for n in range(2):
                link(nc.vector.tensor_tensor(lams[:, 2 * n], lams[:, 2 * n], lams[:, 2 * n + 1], ALU.mult))
                last = nc.vector.tensor_reduce(lam_t[:, n:n + 1], lams[:, 2 * n], axis=X, op=ALU.add)
            last.then_inc(s_dot, 1)
            dve.wait_ge(s_edot, 1)
            nc.vector.scalar_tensor_tensor(lam_t[:, 4:5], lam_t[:, 3:4], -LAMBDA_INIT, lam_t[:, 2:3], ALU.add, ALU.subtract).then_inc(s_lam, 1)
            nc.vector.tensor_scalar(gcol[:, 1:2], gcol[:, 0:1], 0.5 * (1.0 - LAMBDA_INIT), None, ALU.mult).then_inc(s_lam, 1)
            dve.wait_ge(s_gwt_hi, 1)
            nc.vector.tensor_tensor(gwt[:, 1].rearrange("p k e -> p (k e)"), ps[:, 3 * BANK:3 * BANK + KH * EXPERTS],
                                    gwt[:, 0].bitcast(F32).rearrange("p k e -> p (k e)"), ALU.subtract).then_inc(s_gwt, 1)
            for r in range(4):
                c, kh = r // 2, r % 2
                dve.wait_ge(s_xhi, r + 1)
                nc.vector.tensor_tensor(xn_lo[:, kh, c * TH:(c + 1) * TH], bank(4 + r),
                                        xn_hi[:, kh, c * TH:(c + 1) * TH].bitcast(F32), ALU.subtract).then_inc(s_xlo, 1)

            def remainder(r):
                dve.wait_ge(s_part0, r + 1)
                if r >= 4:
                    dve.wait_ge(s_parts, r - 3)
                nc.vector.scalar_tensor_tensor(resid[r % 4], bank(r % 4), D ** -0.5 if r < 4 else 1.0,
                                               stage[r // 2][:, 0, r % 2 * TH:(r % 2 + 1) * TH], ALU.mult, ALU.subtract).then_inc(s_resid, 1)

            sig, sc, masked, sel = table(2), table(3), table(4), table(5)
            for r in range(3):
                remainder(r)
            dve.wait_ge(s_el, 1)
            link(nc.vector.tensor_scalar(small[:, 1], small[:, 1], 1.0, None, ALU.add))
            link(nc.vector.reciprocal(small[:, 2], small[:, 1]))
            remainder(3)
            link(nc.vector.tensor_tensor(sc, sig, bias_b[:, :].rearrange("p (o e) -> p o e", o=1).to_broadcast([P, NT, EXPERTS]), ALU.add))
            gmax = small[:, 6, 0:NT * GROUPS].rearrange("p (i a) -> p i a", a=GROUPS)
            link(nc.vector.tensor_reduce(gmax, small[:, 3].rearrange("p (i a e) -> p i a e", a=GROUPS, e=PER_GROUP), axis=X, op=ALU.max))

            dve.wait_ge(s_const, 2)

            def rank(out, values, n, tmp_a, tmp_b, tile0, tiles):
                shape = [P, tiles, n, n]
                mine = values[:, tile0:tile0 + tiles].rearrange("p i (e o) -> p i e o", o=1).to_broadcast(shape)
                theirs = values[:, tile0:tile0 + tiles].rearrange("p i (o e) -> p i o e", o=1).to_broadcast(shape)
                lower = lower16[:, 0:n, 0:n].rearrange("p (o e) f -> p o e f", o=1).to_broadcast(shape)
                a = tmp_a[:, 0:tiles * n * n].rearrange("p (i e f) -> p i e f", e=n, f=n)
                b = tmp_b[:, 0:tiles * n * n].rearrange("p (i e f) -> p i e f", e=n, f=n)
                nc.vector.tensor_tensor(a, theirs, mine, ALU.is_gt)
                link(nc.vector.tensor_tensor(b, theirs, mine, ALU.is_ge))
                link(nc.vector.tensor_tensor(b, b, lower, ALU.mult))
                link(nc.vector.tensor_tensor(a, a, b, ALU.max))
                link(nc.vector.tensor_reduce(out[:, tile0:tile0 + tiles], a, axis=X, op=ALU.add))

            rank(sel_g, gmax, GROUPS, rank_a, rank_b, 0, NT)
            for r in range(4, 8):
                remainder(r)
            link(nc.vector.tensor_scalar(small[:, 0, 0:NT * GROUPS], small[:, 0, 0:NT * GROUPS], float(TOPG), None, ALU.is_lt))
            link(nc.vector.tensor_scalar(small[:, 6, 0:NT * GROUPS], small[:, 0, 0:NT * GROUPS], 1.0, BIG, ALU.subtract, ALU.mult))

            def by_expert(t):
                return t.rearrange("p (i a o) -> p (i a) o", a=GROUPS, o=1).to_broadcast([P, NT * GROUPS, PER_GROUP])

            m3 = small[:, 4].rearrange("p (i e) -> p i e", e=PER_GROUP)
            link(nc.vector.tensor_tensor(m3, small[:, 3].rearrange("p (i e) -> p i e", e=PER_GROUP), by_expert(small[:, 0, 0:NT * GROUPS]), ALU.mult))
            link(nc.vector.tensor_tensor(m3, m3, by_expert(small[:, 6, 0:NT * GROUPS]), ALU.add))
            rank(sel, masked, EXPERTS, rank_a, rank_b, 0, NT)
            link(nc.vector.tensor_scalar(small[:, 5], small[:, 5], float(TOPK), None, ALU.is_lt))
            link(nc.vector.tensor_tensor(small[:, 5], small[:, 5], small[:, 2], ALU.mult))
            link(nc.vector.tensor_reduce(small[:, 7, 0:NT], sel, axis=X, op=ALU.add))
            link(nc.vector.reciprocal(small[:, 7, NT:2 * NT], small[:, 7, 0:NT]))
            link(nc.vector.tensor_scalar(small[:, 7, NT:2 * NT], small[:, 7, NT:2 * NT], 0.5, None, ALU.mult))
            link(nc.vector.tensor_tensor(sel, sel, small[:, 7, NT:2 * NT].rearrange("p (i o) -> p i o", o=1).to_broadcast([P, NT, EXPERTS]), ALU.mult))
            dve.wait_ge(s_parts, 8)
            dve.wait_ge(s_lam, 2)

            with dve.Fori(0, HALVES) as hf:
                u0 = hf * UNITS
                n0 = hf * STEPS

                def silu(k):
                    m = size_of(k)
                    dve.wait_ge(s_th, u0 + (k + 1 + CREDIT))
                    nc.vector.scalar_tensor_tensor(hid[0:m, k % 2], hid[0:m, k % 2], 1.0, bank(B_UP, rows=m), ALU.add, ALU.mult).then_inc(s_u, 1)

                def hidden(k):
                    m = size_of(k)
                    dve.wait_ge(s_b, u0 + (k + 1 + CREDIT))
                    if k < SHT:
                        dve.wait_ge(s_u, u0 + (k + 1 + CREDIT))
                        nc.vector.scalar_tensor_tensor(hid[0:m, k % 2], hid[0:m, k % 2], 0.5, bank(B_GATE, rows=m), ALU.mult, ALU.mult).then_inc(s_h, 1)
                    else:
                        dve.wait_ge(s_uc, hf * RTILES + (k - SHT + 2))
                        nc.vector.tensor_tensor(hid[0:m, k % 2], hid[0:m, k % 2], bank(B_GATE, rows=m), ALU.mult).then_inc(s_h, 1)

                def maxima(s, c):
                    i = ORDER[s % NT]
                    w = (i + 1) * P
                    at = (B_SCORE + (c if i < 4 else 0)) * BANK
                    dve.wait_ge(s_score, n0 * 2 + (2 * s + c + 1 + CREDIT + 2 * NT))
                    nc.vector.tensor_reduce(negmax[:, s % 4, c:c + 1], ps[:, at:at + w], axis=X, op=ALU.max, negate=True).then_inc(s_negmax, 1)

                def reciprocal(s):
                    dve.wait_ge(s_prob, n0 * 2 + (2 * s + 2 + CREDIT))
                    nc.vector.reciprocal(coef[:, s % 4, 0:1], sums[:, 1, bass.ds(hf, 1), s]).then_inc(s_rsum, 1)

                def coefficient(s):
                    dve.wait_ge(s_rsum, n0 + (s + 1))
                    nc.vector.tensor_scalar(coef[:, s % 4, 1:2], coef[:, s % 4, 0:1], sums[:, 0, bass.ds(hf, 1), s], lam_t[:, 4:5],
                                            ALU.mult, ALU.mult).then_inc(s_coef, 1)

                def combine(s):
                    w = (ORDER[s % NT] + 1) * P
                    dve.wait_ge(s_coef, n0 + (s + 1))
                    nc.vector.scalar_tensor_tensor(probs[:, s % 2, 0, 0:w], probs[:, s % 2, 1, 0:w], coef[:, s % 4, 1:2], probs[:, s % 2, 0, 0:w],
                                                   ALU.mult, ALU.add).then_inc(s_comb, 1)

                def copy_trans(s, grp):
                    gi = FIRST_GROUP[s] + grp
                    w = min(BANK, (ORDER[s % NT] + 1 - 4 * grp) * P)
                    dve.wait_ge(s_athi, hf * GPH + (gi + 1 + CREDIT))
                    nc.vector.tensor_tensor(at_lo[:, gi % 2, 0:w], ps[:, B_TRANS * BANK:B_TRANS * BANK + w],
                                            at_hi[:, gi % 2, 0:w].bitcast(F32), ALU.subtract).then_inc(s_atlo, 1)

                def low_values():
                    dve.wait_ge(s_vhi, hf + 1)
                    nc.vector.tensor_tensor(v_lo[:, :, :], v_all[:, :, bass.ds(hf * P, P)], v_hi[:, :, :].bitcast(F32), ALU.subtract).then_inc(s_vlo, 1)

                dve.wait_ge(s_uc, hf * RTILES + 1)
                nc.vector.tensor_copy(cw_rep[:, :, :].rearrange("p i (e q) -> p (i e) q", q=Q),
                                      small[:, 5, bass.ds(hf * (TH // P * EXPERTS), TH // P * EXPERTS)].rearrange("p (n o) -> p n o", o=1)
                                      .to_broadcast([P, TH // P * EXPERTS, Q])).then_inc(s_cwrep, 1)
                for part, n in order["dve"]:
                    if part == "silu":
                        silu(n)
                    elif part == "hidden":
                        hidden(n)
                    elif part == "v_lo":
                        low_values()
                    elif part == "maxima":
                        maxima(*divmod(n, 2))
                    elif part == "reciprocal":
                        reciprocal(n)
                    elif part == "coefficient":
                        coefficient(n)
                    elif part == "combine":
                        combine(n)
                    elif part == "trans_lo":
                        copy_trans(*GROUP[n])
                dve.wait_ge(s_accth, hf + 1)
                nc.vector.scalar_tensor_tensor(gate[:, bass.ds(hf * 4, 4)].rearrange("p i e -> p (i e)"), probs[:, 0, 0], 1.0, bank(B_ACC, 2),
                                               ALU.add, ALU.mult).then_inc(s_accfree, 1)

            dve.wait_ge(s_w13lo, HALVES * UNITS + 2 + CREDIT)
            dve.wait_ge(s_w13hi, HALVES * UNITS + 2 + CREDIT)
            link(nc.vector.memset(head_ones, 0.0))
            for n in range(HH):
                last = nc.vector.memset(tail[n * DV:(n + 1) * DV, 10496 + n:10497 + n], 1.0 / DV)
            last.then_inc(s_fac, 1)
            l1 = sums[:, 0].rearrange("p f (h i) -> p f h i", i=NT)
            link(nc.vector.tensor_tensor(fac[:, 0], l1, l1, ALU.mult))
            for hf in range(HALVES):
                dve.wait_ge(s_ss, hf + 1)
                for pos, i in enumerate(ORDER):
                    src = ps[:, (4 + hf) * BANK + i * HH:(4 + hf) * BANK + (i + 1) * HH]
                    last = nc.vector.scalar_tensor_tensor(fac[:, 1, hf, :, pos], fac[:, 0, hf, :, pos], EPS, src, ALU.mult, ALU.add)
                last.then_inc(s_fac, 1)
                dve.wait_ge(s_sdf, hf + 1)
                link(nc.vector.reciprocal(fac[:, 2, hf], fac[:, 2, hf]))
                link(nc.vector.tensor_tensor(fac[:, 3, hf], fac[:, 2, hf], fac[:, 2, hf], ALU.mult))
                link(nc.vector.tensor_tensor(fac[:, 3, hf], fac[:, 3, hf], fac[:, 1, hf], ALU.mult))
                link(nc.vector.tensor_scalar(fac[:, 3, hf], fac[:, 3, hf], -0.5, 1.5, ALU.mult, ALU.add))
                link(nc.vector.tensor_tensor(fac[:, 2, hf], fac[:, 2, hf], fac[:, 3, hf], ALU.mult))
                for pos, i in enumerate(ORDER):
                    last = nc.vector.tensor_copy(frep[:, hf, i], fac[:, 2, hf, :, pos].rearrange("p (h o) -> p h o", o=1).to_broadcast([P, HH, DV]))
                last.then_inc(s_frep, 1)

            def norm_lo(hf):
                dve.wait_ge(s_onhi, hf + 1)
                nc.vector.tensor_tensor(xn_lo[:, hf], normed[:, hf], xn_hi[:, hf].bitcast(F32), ALU.subtract).then_inc(s_onlo, 1)

            def norm(hf):
                dve.wait_ge(s_fps, hf + 1)
                nc.vector.scalar_tensor_tensor(normed[:, hf], ot[:, hf], gcol[:, 1:2], bank(2 * hf, 2), ALU.mult, ALU.mult).then_inc(s_on, 1)

            norm(0)
            norm_lo(0)
            norm(1)
            norm_lo(1)
            dve.wait_ge(s_xre, 16)
            for r in range(4):
                two = slice(2 * r, 2 * r + 2)
                dve.wait_ge(s_so, r + 1)
                nc.vector.tensor_tensor(result[:, two], gate[:, two], bank(4 + r).rearrange("p (i e) -> p i e", e=E), ALU.mult).then_inc(s_gated, 1)
                if r % 2 == 1:
                    dve.wait_ge(s_gated, r + 1)
                    nc.vector.tensor_tensor(result[:, two], result[:, two], x_again[:, two], ALU.add).then_inc(s_res_v, 1)

        @block.gpsimd
        def _(pool):
            links = [0]

            def link(ins):
                links[0] += 1
                ins.then_inc(s_link_p, 1)
                pool.wait_ge(s_link_p, links[0])

            for s in (s_w13lo, s_w2lo, s_hlo):
                pool.sem_inc(s, CREDIT)
            pool.sem_inc(s_uc, 1)
            link(pool.memset(ident[:, :], 0.0))
            pool.affine_select(out=ident[:, :], in_=ident[:, :], compare_op=ALU.not_equal, fill=1.0, base=0,
                               pattern=[[-1, P]], channel_multiplier=1).then_inc(s_const, 1)
            link(pool.memset(lower16[:, :, :], 1.0))
            link(pool.affine_select(out=lower16[:, :, :], in_=lower16[:, :, :], compare_op=ALU.is_ge, fill=0.0, base=-1,
                                    pattern=[[1, EXPERTS], [-1, EXPERTS]], channel_multiplier=0))
            link(pool.memset(ident_bf[:, :], 0.0))
            link(pool.affine_select(out=ident_bf[:, :], in_=ident_bf[:, :], compare_op=ALU.not_equal, fill=1.0, base=0,
                                    pattern=[[-1, P]], channel_multiplier=1))
            link(pool.memset(causal[:, :], 0.0))
            pool.affine_select(out=causal[:, :], in_=causal[:, :], compare_op=ALU.is_ge, fill=-BIG, base=0,
                               pattern=[[-1, P]], channel_multiplier=1).then_inc(s_const, 1)

            def split_lo(n):
                slot = (0, 1, 0, 1)[n]
                return pool.tensor_tensor(out=w_ring[:, slot, 1].rearrange("p m n -> p (m n)"), in0=wraw[:, n].rearrange("p k e -> p (k e)"),
                                          in1=w_ring[:, slot, 0].bitcast(F32).rearrange("p m n -> p (m n)"), op=ALU.subtract)

            for n in range(3):
                pool.wait_ge(s_phi, n + 1)
                if n == 2:
                    pool.wait_ge(s_proj, 4)
                split_lo(n).then_inc(s_plo, 1)
                for r in range(4 * n - 4, 4 * n):
                    if r >= 0:
                        pool.wait_ge(s_part1, r + 1)
                        at = slice(r % 2 * TH, (r % 2 + 1) * TH)
                        pool.tensor_tensor(out=stage[r // 2][:, 2, at], in0=resid[r % 4], in1=stage[r // 2][:, 1, at], op=ALU.subtract).then_inc(s_parts, 1)
            pool.wait_ge(s_v, 4)

            def split_w13(k):
                pool.tensor_tensor(out=ring_tile(k, 1), in0=raw_tile(k), in1=ring_tile(k, 0, F32), op=ALU.subtract).then_inc(s_w13lo, 1)

            for k in range(2):
                pool.wait_ge(s_w13hi, k + 1 + CREDIT)
                split_w13(k)

            with pool.Fori(0, HALVES) as hf:
                u0 = hf * UNITS

                def split_w2(k):
                    m = size_of(k)
                    pool.wait_ge(s_w2hi, u0 + (k + 1 + CREDIT))
                    pool.tensor_tensor(out=w2_ring[0:m, k % 2, 1], in0=w2r[0:m, k], in1=w2_ring[0:m, k % 2, 0].bitcast(F32),
                                       op=ALU.subtract).then_inc(s_w2lo, 1)

                def hidden_lo(k):
                    m = size_of(k)
                    pool.wait_ge(s_hhi, u0 + (k + 1 + CREDIT))
                    pool.tensor_tensor(out=h_lo[0:m, k % 2], in0=hid[0:m, k % 2], in1=h_hi[0:m, k % 2].bitcast(F32), op=ALU.subtract).then_inc(s_hlo, 1)

                def weigh(k):
                    if k == SHT:
                        pool.wait_ge(s_cwhalf, hf + 1)
                    pool.wait_ge(s_u, u0 + (k + 1 + CREDIT))
                    pool.tensor_tensor(out=hid[:, k % 2], in0=hid[:, k % 2], in1=cw_half[:, :], op=ALU.mult).then_inc(s_uc, 1)

                for part, n in order["pool"]:
                    if part == "w13_lo":
                        pool.wait_ge(s_w13hi, u0 + (n + 1 + CREDIT))
                        split_w13(n)
                    elif part == "w2_lo":
                        split_w2(n)
                    elif part == "weigh":
                        weigh(n)
                    elif part == "hidden_lo":
                        hidden_lo(n)
                for k in range(2):
                    pool.wait_ge(s_w13hi, u0 + (UNITS + k + 1 + CREDIT))
                    split_w13(k)
            pool.wait_ge(s_wohi, 1)
            split_lo(3).then_inc(s_wolo, 1)
            pool.wait_ge(s_xre, 16)
            for r in (0, 2):
                two = slice(2 * r, 2 * r + 2)
                pool.wait_ge(s_gated, r + 1)
                pool.tensor_tensor(out=result[:, two], in0=result[:, two], in1=x_again[:, two], op=ALU.add).then_inc(s_res_p, 1)


_INS = ["L0_attn_x", "L0_attn_Wq", "L0_attn_Wk", "L0_attn_Wv", "L0_attn_Wo", "L0_attn_lambda_q1", "L0_attn_lambda_k1",
        "L0_attn_lambda_q2", "L0_attn_lambda_k2", "L0_attn_g", "L0_ffn_gate_w", "L0_ffn_expert_bias", "L0_ffn_w1",
        "L0_ffn_w2", "L0_ffn_w3", "L0_ffn_sw1", "L0_ffn_sw2", "L0_ffn_sw3"]


def kernel(**inputs):
    import numpy as _np
    import concourse.bacc as _bacc
    from concourse.bass_utils import run_bass_kernel_spmd as _run

    nc = _bacc.Bacc("TRN2", target_bir_lowering=False, num_devices=1)
    arrays, args = {}, []
    for name in _INS:
        a = _np.ascontiguousarray(inputs[name])
        arrays[name] = a
        args.append(nc.dram_tensor(name, a.shape, mybir.dt.from_np(a.dtype), kind="ExternalInput").ap())
    out = nc.dram_tensor("out", (1, T, E), F32, kind="ExternalOutput").ap()
    build(nc, *args, out)
    r = _run(nc, [arrays], core_ids=[0])
    return r.results[0]["out"]
```
